# Optimizing a Trainium2 kernel written in Bass

```python
import numpy as np
import jax
import jax.numpy as jnp

def _softmax(x, axis=-1):
    return jax.nn.softmax(x, axis=axis)

def _gelu(x):
    return jax.nn.gelu(x, approximate=True)

def _silu(x):
    return jax.nn.silu(x)

def _sigmoid(x):
    return jax.nn.sigmoid(x)

def _layernorm(x, axis=-1, eps=1e-05):
    m = jnp.mean(x, axis=axis, keepdims=True)
    v = jnp.var(x, axis=axis, keepdims=True)
    return (x - m) / jnp.sqrt(v + eps)

def _scatter_add(tgt, idx, src, axis=0):
    return tgt.at[idx].add(src)

def _segment_sum(src, seg, n):
    return jax.ops.segment_sum(src, seg, n)
kernel_name = 'mk_lm_tower_d1_tok_ids1024_r4_c6f0f7'

def setup_inputs(seed: int=0):
    np.random.seed(seed)
    _w = jnp.asarray

    def _rec_inputs():
        import jax
        import jax.numpy as jnp
        _rk = jax.random.key(seed)
        x = jax.random.randint(jax.random.fold_in(_rk, 1), (16, 128), 0, 30521, jnp.int32)
        mask_BS_i2_0 = jnp.where(jnp.ones((16, 128), dtype=bool), 2, 0).astype(jnp.int32)
        return (x, mask_BS_i2_0)
    x, mask_BS_i2_0 = _rec_inputs()

    def _L0_tok_setup():
        import jax, jax.numpy as jnp
        import numpy as np
        LN_EPS = 1e-06
        VOCAB, SEG_VOCAB, MAX_LEN, EMB = (30522, 3, 128, 256)
        B, S = (32, 128)
        key = jax.random.key(seed)
        k1, k2, k3, k4, k5 = jax.random.split(key, 5)
        return {'src': jax.random.randint(k1, (B, S), 0, VOCAB, dtype=jnp.int64 if jax.config.read('jax_enable_x64') else jnp.int32), 'seg': jax.random.randint(k2, (B, S), 0, SEG_VOCAB, dtype=jnp.int64 if jax.config.read('jax_enable_x64') else jnp.int32), 'W_word': jax.random.normal(k3, (VOCAB, EMB), dtype=jnp.float32), 'W_pos': jax.random.normal(k4, (MAX_LEN, EMB), dtype=jnp.float32), 'W_seg': jax.random.normal(k5, (SEG_VOCAB, EMB), dtype=jnp.float32), 'gamma': jnp.ones((EMB,), dtype=jnp.float32), 'beta': jnp.zeros((EMB,), dtype=jnp.float32)}
    _L0_tok_all = _L0_tok_setup()
    _L0_tok_in = {k: v for k, v in _L0_tok_all.items() if k in ('W_word', 'W_pos', 'W_seg', 'gamma', 'beta')}
    del _L0_tok_all

    def _L0_attn_setup():
        import jax, jax.numpy as jnp
        import numpy as np
        import math
        N_HEAD = 16
        N_KV_HEAD = 4
        WINDOW = 128
        EPS = 1e-06

        def _rotate_half(t):
            t1, t2 = jnp.split(t, 2, axis=-1)
            return jnp.concatenate([-t2, t1], axis=-1)

        def _rope_tables(T, head_dim):
            theta = 1.0 / 10000.0 ** (jnp.arange(0, head_dim, 2, dtype=jnp.float32) / head_dim)
            pos = jnp.arange(T, dtype=jnp.float32)
            freqs = jnp.outer(pos, theta)
            cos = jnp.concatenate([jnp.cos(freqs), jnp.cos(freqs)], axis=-1)
            sin = jnp.concatenate([jnp.sin(freqs), jnp.sin(freqs)], axis=-1)
            return (cos, sin)
        key = jax.random.key(seed)
        k1, k2, k3, k4 = jax.random.split(key, 4)
        B, T, C = (1, 512, 256)
        kv_out = 2 * N_KV_HEAD * (C // N_HEAD)
        x = jax.random.normal(k1, (B, T, C), dtype=jnp.float32)
        Wq = jax.random.normal(k2, (C, C), dtype=jnp.float32) * 0.02
        Wkv = jax.random.normal(k3, (kv_out, C), dtype=jnp.float32) * 0.02
        Wproj = jax.random.normal(k4, (C, C), dtype=jnp.float32) * 0.02
        return {'x': x, 'Wq': Wq, 'Wkv': Wkv, 'Wproj': Wproj}
    _L0_attn_all = _L0_attn_setup()
    _L0_attn_in = {k: v for k, v in _L0_attn_all.items() if k in ('Wq', 'Wkv', 'Wproj')}
    del _L0_attn_all

    def _L0_ffn_setup():
        import jax, jax.numpy as jnp
        import numpy as np
        D_MODEL = 256
        N_EXPERTS = 8
        TOP_K = 2
        key = jax.random.key(seed)
        ks = jax.random.split(key, 8)
        d, e = (D_MODEL, N_EXPERTS)
        s = 1.0 / np.sqrt(d)
        return {'x': jax.random.normal(ks[0], (4, 512, d), dtype=jnp.float32), 'W_gate': jax.random.uniform(ks[1], (d, e), jnp.float32, -s, s), 'b_gate': jax.random.uniform(ks[2], (e,), jnp.float32, -s, s), 'W1': jax.random.uniform(ks[3], (e, d, d), jnp.float32, -s, s), 'b1': jax.random.uniform(ks[4], (e, d), jnp.float32, -s, s), 'W2': jax.random.uniform(ks[5], (e, d, d), jnp.float32, -s, s), 'b2': jax.random.uniform(ks[6], (e, d), jnp.float32, -s, s)}
    _L0_ffn_all = _L0_ffn_setup()
    _L0_ffn_in = {k: v for k, v in _L0_ffn_all.items() if k in ('W_gate', 'b_gate', 'W1', 'b1', 'W2', 'b2')}
    del _L0_ffn_all
    return {'x': x, 'mask_BS_i2_0': mask_BS_i2_0, 'L0_tok_W_word': _L0_tok_in['W_word'], 'L0_tok_W_pos': _L0_tok_in['W_pos'], 'L0_tok_W_seg': _L0_tok_in['W_seg'], 'L0_tok_gamma': _L0_tok_in['gamma'], 'L0_tok_beta': _L0_tok_in['beta'], 'L0_attn_Wq': _L0_attn_in['Wq'], 'L0_attn_Wkv': _L0_attn_in['Wkv'], 'L0_attn_Wproj': _L0_attn_in['Wproj'], 'L0_ffn_W_gate': _L0_ffn_in['W_gate'], 'L0_ffn_b_gate': _L0_ffn_in['b_gate'], 'L0_ffn_W1': _L0_ffn_in['W1'], 'L0_ffn_b1': _L0_ffn_in['b1'], 'L0_ffn_W2': _L0_ffn_in['W2'], 'L0_ffn_b2': _L0_ffn_in['b2']}

def reference(x, mask_BS_i2_0, L0_tok_W_word, L0_tok_W_pos, L0_tok_W_seg, L0_tok_gamma, L0_tok_beta, L0_attn_Wq, L0_attn_Wkv, L0_attn_Wproj, L0_ffn_W_gate, L0_ffn_b_gate, L0_ffn_W1, L0_ffn_b1, L0_ffn_W2, L0_ffn_b2):
    import jax
    import jax.numpy as jnp

    def _L0_tok_ref(src, seg, W_word, W_pos, W_seg, gamma, beta):
        import jax, jax.numpy as jnp
        import numpy as np
        LN_EPS = 1e-06
        VOCAB, SEG_VOCAB, MAX_LEN, EMB = (30522, 3, 128, 256)
        B, S = (32, 128)
        seq_len = src.shape[1]
        emb = W_word[src] + W_pos[:seq_len][None, :, :] + W_seg[seg]
        mu = jnp.mean(emb, axis=-1, keepdims=True)
        var = jnp.mean(jnp.square(emb - mu), axis=-1, keepdims=True)
        out = (emb - mu) * jax.lax.rsqrt(var + LN_EPS) * gamma + beta
        return out

    def _L0_attn_ref(x, Wq, Wkv, Wproj):
        import jax, jax.numpy as jnp
        import numpy as np
        import math
        N_HEAD = 16
        N_KV_HEAD = 4
        WINDOW = 128
        EPS = 1e-06

        def _rotate_half(t):
            t1, t2 = jnp.split(t, 2, axis=-1)
            return jnp.concatenate([-t2, t1], axis=-1)

        def _rope_tables(T, head_dim):
            theta = 1.0 / 10000.0 ** (jnp.arange(0, head_dim, 2, dtype=jnp.float32) / head_dim)
            pos = jnp.arange(T, dtype=jnp.float32)
            freqs = jnp.outer(pos, theta)
            cos = jnp.concatenate([jnp.cos(freqs), jnp.cos(freqs)], axis=-1)
            sin = jnp.concatenate([jnp.sin(freqs), jnp.sin(freqs)], axis=-1)
            return (cos, sin)
        B, T, C = x.shape
        H, KV = (N_HEAD, N_KV_HEAD)
        d = C // H
        n_rep = H // KV
        q = (x @ Wq.T).reshape(B, T, H, d).transpose(0, 2, 1, 3)
        kv = x @ Wkv.T
        k, v = jnp.split(kv, 2, axis=2)
        k = k.reshape(B, T, KV, d).transpose(0, 2, 1, 3)
        v = v.reshape(B, T, KV, d).transpose(0, 2, 1, 3)
        q = q / (jnp.linalg.norm(q, axis=-1, keepdims=True) + EPS)
        k = k / (jnp.linalg.norm(k, axis=-1, keepdims=True) + EPS)
        cos, sin = _rope_tables(T, d)
        cos = cos[None, None]
        sin = sin[None, None]
        q = q * cos + _rotate_half(q) * sin
        k = k * cos + _rotate_half(k) * sin
        k = jnp.repeat(k, n_rep, axis=1)
        v = jnp.repeat(v, n_rep, axis=1)
        rows = jnp.arange(T)[:, None]
        cols = jnp.arange(T)[None, :]
        mask = (cols <= rows) & (cols > rows - WINDOW)
        scale = 1.0 / math.sqrt(d)
        scores = jnp.einsum('bhqd,bhkd->bhqk', q, k) * scale
        scores = jnp.where(mask[None, None], scores, -jnp.inf)
        attn = jax.nn.softmax(scores, axis=-1)
        y = jnp.einsum('bhqk,bhkd->bhqd', attn, v)
        y = y.transpose(0, 2, 1, 3).reshape(B, T, C)
        return y @ Wproj.T

    def _L0_ffn_ref(x, W_gate, b_gate, W1, b1, W2, b2):
        import jax, jax.numpy as jnp
        import numpy as np
        D_MODEL = 256
        N_EXPERTS = 8
        TOP_K = 2
        B, T, d = x.shape
        xf = x.reshape(-1, d)
        scores = xf @ W_gate + b_gate
        topk_val, topk_idx = jax.lax.top_k(scores, TOP_K)
        onehot = jax.nn.one_hot(topk_idx, N_EXPERTS, dtype=xf.dtype)
        w = jnp.einsum('nk,nke->ne', topk_val, onehot)
        h = jax.nn.relu(jnp.einsum('nd,edh->neh', xf, W1) + b1)
        y = jnp.einsum('neh,ehd->ned', h, W2) + b2
        out = jnp.einsum('ned,ne->nd', y, w)
        return out.reshape(B, T, d)
    h = _L0_tok_ref(x, mask_BS_i2_0, L0_tok_W_word, L0_tok_W_pos, L0_tok_W_seg, L0_tok_gamma, L0_tok_beta)
    h = h + _L0_attn_ref(_layernorm(h, axis=-1), L0_attn_Wq, L0_attn_Wkv, L0_attn_Wproj)
    h = h + _L0_ffn_ref(_layernorm(h, axis=-1), L0_ffn_W_gate, L0_ffn_b_gate, L0_ffn_W1, L0_ffn_b1, L0_ffn_W2, L0_ffn_b2)
    return h

_drawn_inputs = setup_inputs


def setup_inputs(seed=0):
    import zlib

    import numpy as np

    out = dict(_drawn_inputs(seed))
    spreads = {'L0_tok_gamma': (1.0, 0.2), 'L0_tok_beta': (0.0, 0.1)}
    factors = {'L0_attn_Wq': 8.0, 'L0_ffn_b1': 2.719}
    for name, (base, spread) in spreads.items():
        noise = np.random.default_rng([zlib.crc32(name.encode()), seed]).standard_normal(out[name].shape)
        drawn = base * np.exp(spread * noise) if base else spread * noise
        out[name] = jnp.asarray(drawn.astype(out[name].dtype))
    for name, factor in factors.items():
        out[name] = (out[name] * factor).astype(out[name].dtype)
    return out
```

```python
from contextlib import ExitStack

import numpy as np

import concourse.bass as bass
from concourse import mybir

ALU = mybir.AluOpType
ACT = mybir.ActivationFunctionType
F32 = mybir.dt.float32
F32R = mybir.dt.float32r
BF16 = mybir.dt.bfloat16
I32 = mybir.dt.int32
U32 = mybir.dt.uint32
AX_X = mybir.AxisListType.X

P = 128
SEQS = 16
PAIRS = SEQS // 2
D = 256
KC = D // P
HEADS, KVH, HD = 16, 4, 16
REP = HEADS // KVH
QK = (HEADS + KVH) * HD
QKV = QK + KVH * HD
EXPERTS, TOPK = 8, 2
TOKENS = SEQS * P
CAP = TOKENS + P
SLOTS = TOKENS * TOPK // P + EXPERTS - 1
SPARE = EXPERTS - 1
ROW = D + 2
NO_TOKEN = float(1 << 20)
LN_EPS, NORM_EPS, TOK_EPS = 1e-5, 1e-6, 1e-6
MASKED = -30000.0
PADV = 160

LN_STEPS, NORM_STEPS, ROPE_STEPS, STAGE_STEPS = 14, 6, 4, 5
ROUTE_STEPS, CHOSEN_STEPS, TABLE_STEPS = 10, 2, 14
XBUF, YBUF, CBUF, RBUF = 4, 4, 4, 2

C_ID, C_COS, C_SIN = 0, 128, 144
C_ECAP, C_EID = 160, 168
C_SLOT = 176
C_THR = C_SLOT + SLOTS
C_TRI = C_THR + SEQS
C_TOK = C_TRI + EXPERTS * EXPERTS
C_HALF = C_TOK + SEQS
C_WIDTH = C_HALF + 2
B_ID, B_BEFORE, B_ONES, B_MASK = 0, 128, 256, 384
B_WIDTH = 384 + REP * P


def attention_moe_program(nc, x_idx, seg_idx, w_word, w_pos, w_seg, gamma, beta, w_qkv, w_proj,
                          w_gate, b_gate, w1, b1, w2, b2, consts, consts_bf, out):
    x_rows = nc.dram_tensor("x_rows", (EXPERTS * CAP + SPARE * P, ROW), F32).ap()
    y_rows = nc.dram_tensor("y_rows", (TOPK * TOKENS, D), F32).ap()

    with ExitStack() as ctx:
        def sb(name, shape, dt=F32):
            return ctx.enter_context(nc.sbuf_tensor(name, shape, dt))

        def sem(name):
            return ctx.enter_context(nc.semaphore(name))

        cf = sb("cf", [P, C_WIDTH])
        cb = sb("cb", [P, B_WIDTH], BF16)
        ident = cf[:, C_ID:C_ID + P]
        gam = sb("gam", [P, D])
        bet = sb("bet", [P, D])
        bg = sb("bg", [P, EXPERTS])
        widx = sb("widx", [P, SEQS], I32)
        sidx = sb("sidx", [P, SEQS], I32)
        h = sb("h", [P, SEQS, D])
        rows = sb("rows", [P, 2 * RBUF, ROW])
        raw = sb("raw", [P, KC, EXPERTS, D])
        wq_hi = sb("wq_hi", [P, KC, QKV], F32R)
        wq_lo = sb("wq_lo", [P, KC, QKV], F32R)
        wp_hi = sb("wp_hi", [P, KC, D], F32R)
        wp_lo = sb("wp_lo", [P, KC, D], F32R)
        wg = sb("wg", [P, KC, EXPERTS])
        w1_hi = sb("w1_hi", [P, KC, EXPERTS * D], F32R)
        w1_lo = sb("w1_lo", [P, KC, EXPERTS * D], F32R)
        w2_hi = sb("w2_hi", [P, KC, EXPERTS * D], F32R)
        w2_lo = sb("w2_lo", [P, KC, EXPERTS * D], F32R)
        half = sb("half", [P, 2])

        bn = sb("bn", [P, 2, 6])
        mv = sb("mv", [P, 2, 2])
        rstd = sb("rstd", [P, 2])
        var_e = sb("var_e", [P, 2])
        xn = sb("xn", [P, 2, 2, D])
        xT_hi = sb("xT_hi", [P, KC, 2, P], F32R)
        xT_lo = sb("xT_lo", [P, KC, 2, P], F32R)
        sq = sb("sq", [P, 2, QK])
        ss = sb("ss", [P, 2 * (HEADS + KVH)])
        lnss = sb("lnss", [P, 2 * (HEADS + KVH)])
        nrm = sb("nrm", [P, 2 * (HEADS + KVH)])
        inv = sb("inv", [P, 2 * (HEADS + KVH)])
        rn = sb("rn", [P, 2 * (HEADS + KVH)])
        qcos = sb("qcos", [P, 2, QK])
        qsin = sb("qsin", [P, 2, QK])
        qst = sb("qst", [P, 2, 2, HEADS, 4 * HD], F32R)
        kst = sb("kst", [P, 2, 2, KVH, 4 * HD], F32R)
        vz = sb("vz", [P, 2, 2, KVH * PADV])
        kpad = sb("kpad", [P, 2, KVH, P], F32R)
        qT = sb("qT", [P, 2, 2, REP * P], F32R)
        prob = sb("prob", [P, 2, KVH, REP * P])
        yd = sb("yd", [P, 2, REP * P])
        rden = sb("rden", [P, 2 * HEADS])
        y = sb("y", [P, 2, D])
        yT_hi = sb("yT_hi", [P, KC, 2, P], F32R)
        yT_lo = sb("yT_lo", [P, KC, 2, P], F32R)
        x2T = sb("x2T", [P, KC, 2, P])
        sco = sb("sco", [P, 2, EXPERTS])
        top = sb("top", [P, SEQS, 8])
        topi = sb("topi", [P, 2, 8], U32)
        topf = sb("topf", [P, 2, TOPK])
        pick = sb("pick", [P, 2, TOPK, EXPERTS])
        chosen = sb("chosen", [P, 2, EXPERTS], BF16)
        seen = sb("seen", [P, 2, EXPERTS], BF16)
        place = sb("place", [P, 2, EXPERTS])
        picked = sb("picked", [P, 2, TOPK, EXPERTS])
        destf = sb("destf", [P, 2, TOPK])
        dest = sb("dest", [P, SEQS, TOPK], I32)
        pad_rows = sb("pad_rows", [P, ROW])
        bn3 = sb("bn3", [P, 2, 6])
        mv3 = sb("mv3", [P, 2, 2])
        rstd3 = sb("rstd3", [P, 2])
        var3 = sb("var3", [P, 2])
        cnt = sb("cnt", [P, EXPERTS])
        over = sb("over", [P, EXPERTS, SEQS])
        tiles = sb("tiles", [P, EXPERTS])
        before_e = sb("before_e", [P, EXPERTS, EXPERTS])
        ends = sb("ends", [P, EXPERTS])
        slot_e = sb("slot_e", [P, SLOTS])
        slot_0 = sb("slot_0", [P, SLOTS])
        slot_r = sb("slot_r", [P, SLOTS])
        slot_row = sb("slot_row", [P, SLOTS], I32)
        slot_col = sb("slot_col", [P, SLOTS], I32)
        pad_row = sb("pad_row", [P, EXPERTS], I32)
        second = sb("second", [P, YBUF])
        to_row = sb("to_row", [P, YBUF], I32)

        ps = ctx.enter_context(nc.psum_tensor("ps", [P, 8, 512], F32))

        s_const = sem("s_const")
        s_idx = sem("s_idx")
        s_pos = [sem(f"s_pos{n}") for n in range(4)]
        s_word = [sem(f"s_word{t}") for t in range(SEQS)]
        s_emb = [sem(f"s_emb{t}") for t in range(SEQS)]
        s_wraw = sem("s_wraw")
        s_w1raw, s_w2raw = sem("s_w1raw"), sem("s_w2raw")
        s_hi, s_split_hi, s_split = sem("s_hi"), sem("s_split_hi"), sem("s_split")
        s_half, s_seen0, s_nred, s_root = sem("s_half"), sem("s_seen0"), sem("s_nred"), sem("s_root")
        s_qhi = sem("s_qhi")
        s_place, s_picked, s_rstd3 = sem("s_place"), sem("s_picked"), sem("s_rstd3")
        s_init = sem("s_init")
        s_ln = sem("s_ln")
        s_rstd = sem("s_rstd")
        s_xn = sem("s_xn")
        s_xTp, s_xThi, s_xTlo = sem("s_xTp"), sem("s_xThi"), sem("s_xTlo")
        s_qkv = sem("s_qkv")
        s_sq, s_rope, s_norm, s_v = sem("s_sq"), sem("s_rope"), sem("s_norm"), sem("s_v")
        s_stage = sem("s_stage")
        s_kTp, s_kT = sem("s_kTp"), sem("s_kT")
        s_qTp, s_qT = sem("s_qTp"), sem("s_qT")
        s_score, s_prob = sem("s_score"), sem("s_prob")
        s_pv, s_yd = sem("s_pv"), sem("s_yd")
        s_ydT, s_y = sem("s_ydT"), sem("s_y")
        s_yTp, s_yThi, s_yTlo = sem("s_yTp"), sem("s_yThi"), sem("s_yTlo")
        s_proj, s_res = sem("s_proj"), sem("s_res")
        s_ln3, s_x2 = sem("s_ln3"), sem("s_x2")
        s_x2Tp, s_x2T = sem("s_x2Tp"), sem("s_x2T")
        s_gate, s_route, s_chosen, s_before, s_dest = (sem("s_gate"), sem("s_route"), sem("s_chosen"),
                                                       sem("s_before"), sem("s_dest"))
        s_scat = [sem(f"s_scat{n}") for n in range(RBUF)]
        s_before_all, s_table = sem("s_before_all"), sem("s_table")
        s_padded, s_pads = sem("s_padded"), sem("s_pads")
        s_bias = sem("s_bias")
        s_slot = [sem(f"s_slot{n}") for n in range(XBUF)]
        s_sxp, s_sxhi, s_sxlo = sem("s_sxp"), sem("s_sxhi"), sem("s_sxlo")
        s_up, s_hid = sem("s_up"), sem("s_hid")
        s_hTp, s_hThi, s_hTlo = sem("s_hTp"), sem("s_hThi"), sem("s_hTlo")
        s_down, s_ys = sem("s_down"), sem("s_ys")
        s_isk, s_to = sem("s_isk"), sem("s_to")
        s_sent = [sem(f"s_sent{n}") for n in range(YBUF)]
        s_back = [sem(f"s_back{n}") for n in range(CBUF)]
        s_mix, s_out = sem("s_mix"), sem("s_out")

        def bc(ap, n, axis):
            ap = ap.unsqueeze(axis)
            shape = list(ap.shape)
            shape[axis] = n
            return ap.broadcast_to(shape)

        def part(t, *shape):
            flat = t.rearrange("p a c -> p (a c)") if len(t.shape) == 3 else t.rearrange("p b a c -> p (b a c)")
            return flat[:, 0:shape[0] * shape[1]].rearrange("p (m n) -> p m n", m=shape[0])

        past, past_n = part(qcos, SLOTS, EXPERTS), part(qsin, SLOTS, EXPERTS)
        slot_x, slot_y, hid = part(vz, XBUF, ROW), part(yd, YBUF, D), y
        prob_c = prob.rearrange("p a g (h n) -> p (a g h n)", h=2).rearrange("p (c k d) -> p c k d", c=2 * CBUF, k=TOPK)
        def bank(n, cols=512):
            return ps[:, n, 0:cols]

        S_BANK, Q_BANK, X_BANK, V_BANK, QKV_BANK = 0, 2, 4, 5, 6
        qk_ps = ps[:, QKV_BANK:QKV_BANK + 2, 0:QK]
        v_ps = ps[:, QKV_BANK:QKV_BANK + 2, QK:QKV].rearrange("p a (g d) -> p a g d", d=HD)
        y_ps = ps[:, Q_BANK:Q_BANK + 2, :].rearrange("p a (s c) -> p a s c", c=2 * HD)
        vz_v = vz.rearrange("p b a (g c) -> p b a g c", c=PADV)
        qk_n = qsin.rearrange("p a n -> p (a n)")
        q_n = qk_n[:, 0:2 * HEADS * HD].rearrange("p (s d) -> p s d", d=HD)
        k_n = qk_n[:, 2 * HEADS * HD:].rearrange("p (s d) -> p s d", d=HD)

        def q_stage(b):
            v = qst[:, b].rearrange("p a s (c l d) -> p (a s) c l d", c=2, l=2)
            return v[:, :, :, 0], v[:, :, :, 1]

        raw_f = raw.rearrange("p k e d -> p (k e d)")
        w1_f = [w1_hi.rearrange("p k n -> p (k n)"), w1_lo.rearrange("p k n -> p (k n)")]
        w2_f = [w2_hi.rearrange("p k n -> p (k n)"), w2_lo.rearrange("p k n -> p (k n)")]
        PIECE = 1024
        SPLIT = {0: [(0, 0)], 1: [(0, 1), (0, 2)], 2: [(0, 3)], 3: [(1, 0)], 4: [(1, 1), (1, 2)], 5: [(1, 3)]}

        ITERATIONS = range(-2, PAIRS + 2)

        def live(p):
            return 0 <= p < PAIRS

        block = ctx.enter_context(nc.Block())

        @block.sync
        def _(sp):
            sp.dma_start(widx[:], x_idx).then_inc(s_idx, 16)
            sp.dma_start(sidx[:], seg_idx).then_inc(s_idx, 16)
            for q in range(4):
                sp.dma_start(h[:, 4 * q:4 * q + 4, :], bc(w_pos, 4, 1)).then_inc(s_pos[q], 16)
            sp.dma_start(cf[:], consts).then_inc(s_const, 16)
            sp.dma_start(gam[:], gamma.partition_broadcast(P)).then_inc(s_const, 16)
            sp.dma_start(bet[:], beta.partition_broadcast(P)).then_inc(s_const, 16)
            sp.dma_start(cb[:], consts_bf).then_inc(s_const, 16)
            sp.dma_start(bg[:], b_gate.partition_broadcast(P)).then_inc(s_const, 16)
            sp.dma_start(wg[:], w_gate.rearrange("(k p) e -> p k e", p=P)).then_inc(s_const, 16)
            sp.wait_ge(s_hi, 4)
            for k in range(KC):
                sp.dma_start(raw[:, k], w1.rearrange("e (k p) d -> k p e d", p=P)[k]).then_inc(s_w1raw, 16)
            sp.wait_ge(s_split, 8)
            for k in range(KC):
                sp.dma_start(raw[:, k], w2.rearrange("e (k p) d -> k p e d", p=P)[k]).then_inc(s_w2raw, 16)
            sp.wait_ge(s_split, 16)
            sp.dma_start(raw[:, 0], b1.partition_broadcast(P)).then_inc(s_bias, 16)
            sp.dma_start(raw[:, 1], b2.partition_broadcast(P)).then_inc(s_bias, 16)

            sp.wait_ge(s_table, TABLE_STEPS)
            for e in range(EXPERTS):
                at = sp.value_load(pad_row[0:1, e:e + 1], min_val=e * CAP, max_val=e * CAP + TOKENS)
                sp.dma_start(x_rows[bass.ds(at, P), :], pad_rows[:]).then_inc(s_pads, 16)
            sp.wait_ge(s_pads, 16 * (EXPERTS + SPARE))
            for n in range(RBUF):
                sp.wait_ge(s_scat[n], 16 * 2 * TOPK * (PAIRS // RBUF))

            def load_slot(s, n):
                row = sp.value_load(slot_row[0:1, bass.ds(s, 1)], min_val=0, max_val=EXPERTS * CAP + (SPARE - 1) * P)
                sp.dma_start(slot_x[:, n, :], x_rows[bass.ds(row, P), :]).then_inc(s_slot[n], 16)

            for s in range(XBUF):
                load_slot(s, s)
            for s in range(XBUF, SLOTS):
                sp.wait_ge(s_sxp, s - XBUF + 1)
                sp.wait_ge(s_to, s - XBUF + 1)
                load_slot(s, s % XBUF)

            for n in range(YBUF):
                sp.wait_ge(s_sent[n], 16 * len(range(n, SLOTS, YBUF)))
            for t in range(SEQS):
                if t >= CBUF:
                    sp.wait_ge(s_mix, 2 * (t - CBUF + 1))
                back = y_rows.rearrange("(k t p) d -> t p k d", k=TOPK, p=P)[t]
                sp.dma_start(prob_c[:, t % CBUF], back).then_inc(s_back[t % CBUF], 16)
            for t in range(SEQS):
                sp.wait_ge(s_mix, 2 * (t + 1))
                sp.dma_start(out[t], h[:, t, :]).then_inc(s_out, 16)
            sp.wait_ge(s_out, 16 * SEQS)

        @block.gpsimd
        def _(pool):
            def gather(t, table, idx, done):
                nc.gpsimd.indirect_dma_start(
                    out=h[:, t, :], out_offset=None, in_=table,
                    in_offset=bass.IndirectOffsetOnAxis(ap=idx[:, t:t + 1], axis=0),
                    compute_op=ALU.add).then_inc(done, 16)

            def words(t):
                pool.wait_ge(s_pos[t // 4], 16)
                gather(t, w_word, widx, s_word[t])

            def segments(t):
                pool.wait_ge(s_word[t], 16)
                gather(t, w_seg, sidx, s_emb[t])

            pool.wait_ge(s_idx, 32)
            for t in range(4):
                words(t)
            for t in range(2):
                segments(t)
            nc.gpsimd.memset(half[:], -0.5).then_inc(s_half, 1)
            nc.gpsimd.memset(pad_rows[:, 0:D], 0.0).then_inc(s_half, 1)
            nc.gpsimd.memset(pad_rows[:, D:D + 1], NO_TOKEN).then_inc(s_half, 1)
            nc.gpsimd.memset(pad_rows[:, D + 1:ROW], 0.0).then_inc(s_half, 1)
            nc.gpsimd.memset(kpad[:].bitcast(F32), 0.0).then_inc(s_init, 1)
            nc.gpsimd.memset(vz[:], 0.0).then_inc(s_half, 1)
            pool.wait_ge(s_half, 5)
            nc.gpsimd.memset(vz_v[:, :, :, :, HD:HD + 1], 1.0).then_inc(s_init, 1)

            def power(out_ap, in_ap, done):
                nc.gpsimd.tensor_tensor(out_ap, in_ap, half[:, 0:2], ALU.pow).then_inc(done, 1)

            sent = 0
            for i in ITERATIONS:
                for t in (2 * (i + 4), 2 * (i + 4) + 1):
                    if 4 <= t < SEQS:
                        words(t)
                if live(i + 2):
                    p = i + 2
                    pool.wait_ge(s_ln, LN_STEPS * p + 5)
                    power(rstd[:], var_e[:], s_rstd)
                for t in (2 * (i + 3), 2 * (i + 3) + 1):
                    if 2 <= t < SEQS:
                        segments(t)
                if live(i + 2):
                    pool.wait_ge(s_ln, LN_STEPS * p + 14)
                    power(rstd[:], var_e[:], s_rstd)
                if live(i - 2):
                    p = i - 2
                    pool.wait_ge(s_dest, p + 1)
                    for t in (2 * p, 2 * p + 1):
                        for k in range(TOPK):
                            nc.gpsimd.indirect_dma_start(
                                out=x_rows, out_offset=bass.IndirectOffsetOnAxis(ap=dest[:, t, k:k + 1], axis=0),
                                in_=rows[:, t % (2 * RBUF), :], in_offset=None).then_inc(s_scat[p % RBUF], 16)
                for w, c in SPLIT.get(i, []):
                    a, b = c * PIECE, (c + 1) * PIECE
                    hi, lo = (w1_f, w2_f)[w]
                    pool.wait_ge(s_split_hi, 4 * w + c + 1)
                    nc.gpsimd.tensor_tensor(lo[:, a:b], raw_f[:, a:b], hi[:, a:b].bitcast(F32),
                                            ALU.subtract).then_inc(s_split, 2)
                if live(i - 1):
                    pool.wait_ge(s_ln3, 5 * i)
                    power(rstd3[:], var3[:], s_rstd3)

            def send(s, n):
                nc.gpsimd.indirect_dma_start(
                    out=y_rows, out_offset=bass.IndirectOffsetOnAxis(ap=to_row[:, n:n + 1], axis=0),
                    in_=slot_y[:, n, :], in_offset=None, bounds_check=TOPK * TOKENS - 1,
                    oob_is_err=False).then_inc(s_sent[n], 16)

            for s in range(SLOTS):
                pool.wait_ge(s_ys, s + 1)
                pool.wait_ge(s_to, s + 1)
                send(s, s % YBUF)

        @block.tensor
        def _(pe):
            def split_product(out_ap, lhs, rhs, start=True, stop=True):
                n = len(lhs)
                for k in range(n):
                    (ah, al), (bh, bl) = lhs[k], rhs[k]
                    nc.tensor.matmul(out_ap, ah, bh, start=start and k == 0, stop=False)
                    nc.tensor.matmul(out_ap, ah, bl, start=False, stop=False)
                    last = nc.tensor.matmul(out_ap, al, bh, start=False, stop=stop and k == n - 1)
                return last

            def transpose_pair(n, src, done):
                for k in range(KC):
                    for a in range(2):
                        c = (2 * k + a) * P
                        last = nc.tensor.transpose(ps[:, n, c:c + P], src(a)[:, k * P:(k + 1) * P], ident)
                last.then_inc(done, 1)

            def q_transposes(p, a):
                for pr in range(2):
                    m = 4 * p + 2 * a + pr
                    if pr == 0:
                        pe.wait_ge(s_stage, STAGE_STEPS * (p + 1))
                    if m >= 2:
                        pe.wait_ge(s_qT, m - 1)
                    for j in range(REP):
                        two = qst[:, p % 2, a, 4 * j + 2 * pr:4 * j + 2 * pr + 2, :].rearrange("p s c -> p (s c)")
                        last = nc.tensor.transpose(ps[:, Q_BANK + pr, j * P:(j + 1) * P], two.bitcast(F32), ident)
                    last.then_inc(s_qTp, 1)

            def k_transposes(p):
                pe.wait_ge(s_stage, STAGE_STEPS * (p + 1))
                if p >= 1:
                    pe.wait_ge(s_yd, 2 * p)
                for a in range(2):
                    for pr in range(2):
                        c = (2 * a + pr) * P
                        keys = kst[:, p % 2, a, 2 * pr:2 * pr + 2, :].rearrange("p g c -> p (g c)").bitcast(F32)
                        last = nc.tensor.transpose(ps[:, V_BANK, c:c + P], keys, ident)
                last.then_inc(s_kTp, 1)

            def scores(p, a):
                for g in range(KVH):
                    m = 8 * p + 4 * a + g
                    if g == 0:
                        pe.wait_ge(s_kT, 2 * (p + 1))
                        pe.wait_ge(s_const, 16 * 6)
                    pe.wait_ge(s_qT, 4 * p + 2 * a + g // 2 + 1)
                    if m >= 2:
                        pe.wait_ge(s_prob, m - 1)
                    o = bank(S_BANK + g % 2)
                    nc.tensor.matmul(o, kpad[:, a, g, :], qT[:, a, g // 2, :], start=True, stop=False)
                    nc.tensor.matmul(o, cb[:, B_ID:B_ID + P], cb[:, B_MASK:B_MASK + REP * P],
                                     start=False, stop=True).then_inc(s_score, 1)

            def values(p, a):
                pe.wait_ge(s_prob, 8 * p + 4 * a + 4)
                if a == 0:
                    pe.wait_ge(s_kT, 2 * (p + 1))
                    pe.wait_ge(s_v, p + 1)
                    pe.wait_ge(s_init, 2)
                else:
                    pe.wait_ge(s_yd, 2 * p + 1)
                for g in range(KVH):
                    last = nc.tensor.matmul(bank(V_BANK), vz[:, p % 2, a, g * P:(g + 1) * P], prob[:, a, g, :],
                                            start=(g == 0), stop=(g == KVH - 1))
                last.then_inc(s_pv, 1)

            def gate(p):
                pe.wait_ge(s_x2T, p + 1)
                if live(p + 2):
                    pe.wait_ge(s_v, p + 3)
                    pe.wait_ge(s_stage, STAGE_STEPS * (p + 3))
                for a in range(2):
                    for k in range(KC):
                        last = nc.tensor.matmul(ps[:, QKV_BANK, EXPERTS * a:EXPERTS * (a + 1)], x2T[:, k, a, :],
                                                wg[:, k, :], start=(k == 0), stop=(k == KC - 1))
                last.then_inc(s_gate, 1)

            def before(p):
                pe.wait_ge(s_chosen, CHOSEN_STEPS * (p + 1))
                o = ps[:, QKV_BANK + 1, 0:2 * EXPERTS]
                nc.tensor.matmul(o, cb[:, B_BEFORE:B_BEFORE + P], chosen.rearrange("p a e -> p (a e)"),
                                 start=True, stop=False)
                nc.tensor.matmul(o, cb[:, B_ONES:B_ONES + P], seen.rearrange("p a e -> p (a e)"),
                                 start=False, stop=True).then_inc(s_before, 1)

            pe.wait_ge(s_const, 16 * 6)
            for i in ITERATIONS:
                if live(i):
                    k_transposes(i)
                    q_transposes(i, 0)
                if live(i - 2):
                    pe.wait_ge(s_x2, 2 * (i - 1))
                    transpose_pair(X_BANK, lambda a: rows[:, 2 * ((i - 2) % RBUF) + a, 0:D], s_x2Tp)
                if live(i):
                    scores(i, 0)
                if live(i - 2):
                    gate(i - 2)
                if live(i - 1):
                    for a in range(2):
                        pe.wait_ge(s_yd, 2 * (i - 1) + a + 1)
                        if a == 0:
                            pe.wait_ge(s_qT, 4 * i + 2 if live(i) else 4 * i)
                        for j in range(REP):
                            last = nc.tensor.transpose(ps[:, Q_BANK + a, j * P:(j + 1) * P],
                                                       yd[:, a, j * P:(j + 1) * P], ident)
                        last.then_inc(s_ydT, 1)
                if live(i + 1):
                    pe.wait_ge(s_xn, 2 * (i + 2))
                    if live(i - 2):
                        pe.wait_ge(s_x2T, i - 1)
                    if live(i - 1 - 1):
                        pe.wait_ge(s_res, i - 1)
                    transpose_pair(X_BANK, lambda a: xn[:, (i + 1) % 2, a, :], s_xTp)
                if live(i - 2):
                    before(i - 2)
                if live(i):
                    values(i, 0)
                if live(i + 1):
                    pe.wait_ge(s_xTlo, i + 2)
                    pe.wait_ge(s_xThi, i + 2)
                    if i == -1:
                        pe.wait_ge(s_hi, 4)
                    if live(i):
                        pe.wait_ge(s_v, i + 1)
                        pe.wait_ge(s_stage, STAGE_STEPS * (i + 1))
                    if live(i - 2):
                        pe.wait_ge(s_place, i - 1)
                        pe.wait_ge(s_route, ROUTE_STEPS * (i - 1))
                    for a in range(2):
                        last = split_product(ps[:, QKV_BANK + a, 0:QKV],
                                             [(xT_hi[:, k, a, :], xT_lo[:, k, a, :]) for k in range(KC)],
                                             [(wq_hi[:, k, :], wq_lo[:, k, :]) for k in range(KC)])
                        last.then_inc(s_qkv, 1)
                if live(i - 1):
                    pe.wait_ge(s_y, 2 * i)
                    if live(i + 1):
                        pass
                    elif live(i - 2):
                        pe.wait_ge(s_x2T, i - 1)
                    transpose_pair(X_BANK, lambda a: y[:, a, :], s_yTp)
                if live(i):
                    q_waits = s_y
                    if i >= 1:
                        pe.wait_ge(q_waits, 2 * i)
                    q_transposes(i, 1)
                    scores(i, 1)
                if live(i - 1):
                    pe.wait_ge(s_yTlo, i)
                    pe.wait_ge(s_yThi, i)
                    for a in range(2):
                        last = split_product(ps[:, X_BANK, a * D:(a + 1) * D],
                                             [(yT_hi[:, k, a, :], yT_lo[:, k, a, :]) for k in range(KC)],
                                             [(wp_hi[:, k, :], wp_lo[:, k, :]) for k in range(KC)])
                        last.then_inc(s_proj, 1)
                if live(i):
                    values(i, 1)

            pe.wait_ge(s_place, PAIRS)
            nc.tensor.matmul(ps[:, QKV_BANK + 1, 0:EXPERTS], cb[:, B_ONES:B_ONES + P], seen[:, 1, :],
                             start=True, stop=False)
            nc.tensor.matmul(ps[:, QKV_BANK + 1, 0:EXPERTS], cb[:, B_ONES:B_ONES + P], chosen[:, 1, :],
                             start=False, stop=True).then_inc(s_before_all, 1)

            SX, SH, ST, SY = 0, 2, 4, 6

            def slot_transposes(s, b, n):
                pe.wait_ge(s_slot[n], (s // XBUF + 1) * 16)
                if s >= 2:
                    pe.wait_ge(s_sxhi, s - 1)
                    pe.wait_ge(s_sxlo, s - 1)
                for k in range(KC):
                    last = nc.tensor.transpose(ps[:, SX + b, k * P:(k + 1) * P], slot_x[:, n, k * P:(k + 1) * P], ident)
                last.then_inc(s_sxp, 1)

            def up(s, b, col):
                pe.wait_ge(s_sxhi, s + 1)
                pe.wait_ge(s_sxlo, s + 1)
                if s >= 2:
                    pe.wait_ge(s_hid, s - 1)
                split_product(ps[:, SH + b, 0:D], [(xT_hi[:, k, b, :], xT_lo[:, k, b, :]) for k in range(KC)],
                              [(w1_hi[:, k, bass.ds(col, D)], w1_lo[:, k, bass.ds(col, D)]) for k in range(KC)]
                              ).then_inc(s_up, 1)

            def hidden_transposes(s, b):
                pe.wait_ge(s_hid, s + 1)
                if s >= 2:
                    pe.wait_ge(s_hThi, s - 1)
                    pe.wait_ge(s_hTlo, s - 1)
                for k in range(KC):
                    last = nc.tensor.transpose(ps[:, ST + b, k * P:(k + 1) * P], hid[:, b, k * P:(k + 1) * P], ident)
                last.then_inc(s_hTp, 1)

            def down(s, b, col):
                pe.wait_ge(s_hThi, s + 1)
                pe.wait_ge(s_hTlo, s + 1)
                if s >= 2:
                    pe.wait_ge(s_ys, s - 1)
                split_product(ps[:, SY + b, 0:D], [(yT_hi[:, k, b, :], yT_lo[:, k, b, :]) for k in range(KC)],
                              [(w2_hi[:, k, bass.ds(col, D)], w2_lo[:, k, bass.ds(col, D)]) for k in range(KC)]
                              ).then_inc(s_down, 1)

            def column(s):
                return pe.value_load(slot_col[0:1, bass.ds(s, 1)], min_val=0, max_val=(EXPERTS - 1) * D)

            pe.wait_ge(s_table, TABLE_STEPS)
            pe.wait_ge(s_split, 16)
            pe.wait_ge(s_split_hi, 8)
            for s in range(-1, SLOTS + 1):
                if s + 1 < SLOTS:
                    slot_transposes(s + 1, (s + 1) % 2, (s + 1) % XBUF)
                if s >= 1:
                    down(s - 1, (s - 1) % 2, column(s - 1))
                if 0 <= s < SLOTS:
                    hidden_transposes(s, s % 2)
                if s + 1 < SLOTS:
                    up(s + 1, (s + 1) % 2, column(s + 1))

        @block.scalar
        def _(act):
            act.dma_start(raw_f[:, 0:KC * QKV].rearrange("p (k n) -> p k n", k=KC),
                          w_qkv.rearrange("(k p) n -> p k n", p=P)).then_inc(s_wraw, 16)
            act.dma_start(raw_f[:, KC * QKV:KC * (QKV + D)].rearrange("p (k n) -> p k n", k=KC),
                          w_proj.rearrange("(k p) n -> p k n", p=P)).then_inc(s_wraw, 16)
            act.wait_ge(s_half, 4)
            for n in range(SPARE):
                act.dma_start(x_rows[EXPERTS * CAP + n * P:EXPERTS * CAP + (n + 1) * P, :],
                              pad_rows[:]).then_inc(s_pads, 16)

            def copy(out_ap, in_ap, done):
                nc.scalar.activation(out_ap, in_ap, ACT.Copy).then_inc(done, 1)

            def x_bank(n=X_BANK):
                return ps[:, n, :].rearrange("p (k a t) -> p k a t", k=KC, a=2)

            def q_copies(p, a):
                for pr in range(2):
                    m = 4 * p + 2 * a + pr
                    act.wait_ge(s_qTp, m + 1)
                    if p >= 1:
                        act.wait_ge(s_score, 8 * (p - 1) + 4 * a + 2 * pr + 2)
                    copy(qT[:, a, pr, :], bank(Q_BANK + pr), s_qT)

            def probabilities(p, a):
                for g in range(KVH):
                    m = 8 * p + 4 * a + g
                    act.wait_ge(s_score, m + 1)
                    if p >= 1 and g == 0:
                        act.wait_ge(s_pv, 2 * (p - 1) + a + 1)
                    nc.scalar.activation(prob[:, a, g, :], bank(S_BANK + g % 2), ACT.Exp,
                                         scale=float(HD) ** -0.5).then_inc(s_prob, 1)

            def outputs(p, a):
                act.wait_ge(s_pv, 2 * p + a + 1)
                if p >= 1:
                    act.wait_ge(s_ydT, 2 * (p - 1) + a + 1)
                copy(yd[:, a, :], bank(V_BANK), s_yd)

            for i in ITERATIONS:
                if live(i):
                    act.wait_ge(s_kTp, i + 1)
                    if i == 0:
                        act.wait_ge(s_init, 2)
                    if i >= 1:
                        act.wait_ge(s_score, 8 * i)
                    kT = bank(V_BANK).rearrange("p (a r t) -> p a r t", a=2, r=2)
                    kp = kpad.rearrange("p a (r o) t -> p a r o t", o=2)
                    copy(kp[0:64, :, :, 0, :], kT[0:64], s_kT)
                    copy(kp[64:128, :, :, 1, :], kT[64:128], s_kT)
                    q_copies(i, 0)
                if live(i - 2):
                    act.wait_ge(s_x2Tp, i - 1)
                    if i >= 3:
                        act.wait_ge(s_gate, i - 2)
                    copy(x2T[:], x_bank(), s_x2T)
                if live(i):
                    probabilities(i, 0)
                if live(i + 1):
                    p = i + 1
                    act.wait_ge(s_xTp, p + 1)
                    if p >= 1:
                        act.wait_ge(s_qkv, 2 * p)
                        act.wait_ge(s_xTlo, p)
                    copy(xT_hi[:], x_bank(), s_xThi)
                if live(i):
                    outputs(i, 0)
                if live(i + 1):
                    act.wait_ge(s_qkv, 2 * (p + 1))
                    if p >= 1:
                        act.wait_ge(s_stage, STAGE_STEPS * p)
                    nc.scalar.activation(sq[:], qk_ps, ACT.Square).then_inc(s_sq, 1)
                    if p >= 2:
                        act.wait_ge(s_pv, 2 * (p - 1))
                    if p == 0:
                        act.wait_ge(s_init, 2)
                    copy(vz_v[:, p % 2, :, :, 0:HD], v_ps, s_v)
                if live(i - 1):
                    act.wait_ge(s_yTp, i)
                    if i >= 2:
                        act.wait_ge(s_proj, 2 * (i - 1))
                        act.wait_ge(s_yTlo, i - 1)
                    copy(yT_hi[:], x_bank(), s_yThi)
                if live(i + 1):
                    act.wait_ge(s_norm, NORM_STEPS * p + 1)
                    nc.scalar.activation(lnss[:], ss[:], ACT.Ln).then_inc(s_root, 1)
                    act.wait_ge(s_root, 2 * p + 1)
                    nc.scalar.activation(nrm[:], lnss[:], ACT.Exp, scale=0.5).then_inc(s_root, 1)
                    act.wait_ge(s_stage, STAGE_STEPS * p + 2)
                    if p >= 2:
                        act.wait_ge(s_qTp, 4 * (p - 1))
                    copy(q_stage(p % 2)[0], bc(q_n, 2, 2), s_qhi)
                if live(i):
                    q_copies(i, 1)
                    probabilities(i, 1)
                for w, c in SPLIT.get(i, []):
                    a, b = c * PIECE, (c + 1) * PIECE
                    act.wait_ge((s_w1raw, s_w2raw)[w], 16 * KC)
                    copy((w1_f, w2_f)[w][0][:, a:b], raw_f[:, a:b], s_split_hi)
                if live(i):
                    outputs(i, 1)

            def slot_copy(dst, n, done):
                copy(dst, ps[:, n, 0:D].rearrange("p (k t) -> p k t", k=KC), done)

            act.wait_ge(s_table, TABLE_STEPS)
            for s in range(-1, SLOTS):
                if s + 1 < SLOTS:
                    b = (s + 1) % 2
                    act.wait_ge(s_sxp, s + 2)
                    if s + 1 >= 2:
                        act.wait_ge(s_up, s)
                        act.wait_ge(s_sxlo, s)
                    slot_copy(xT_hi[:, :, b, :], 0 + b, s_sxhi)
                if s >= 0:
                    b = s % 2
                    act.wait_ge(s_hTp, s + 1)
                    if s >= 2:
                        act.wait_ge(s_down, s - 1)
                        act.wait_ge(s_hTlo, s - 1)
                    nc.scalar.activation(yT_hi[:, :, b, :], ps[:, 4 + b, 0:D].rearrange("p (k t) -> p k t", k=KC),
                                         ACT.Relu).then_inc(s_hThi, 1)

        @block.vector
        def _(dve):
            V = nc.vector

            def lo_part(dst, n, hi, done):
                V.tensor_tensor(dst, ps[:, n, :].rearrange("p (k a t) -> p k a t", k=KC, a=2), hi.bitcast(F32),
                                ALU.subtract).then_inc(done, 1)

            dve.wait_ge(s_wraw, 32)
            for n, (hi, lo, a, b) in enumerate(((wq_hi, wq_lo, 0, KC * QKV), (wp_hi, wp_lo, KC * QKV, KC * (QKV + D)))):
                V.tensor_copy(hi.rearrange("p k n -> p (k n)"), raw_f[:, a:b]).then_inc(s_hi, 1)
                dve.wait_ge(s_hi, 2 * n + 1)
                V.tensor_tensor(lo.rearrange("p k n -> p (k n)"), raw_f[:, a:b],
                                hi.rearrange("p k n -> p (k n)").bitcast(F32), ALU.subtract).then_inc(s_hi, 1)
            V.memset(seen[:], 0.0).then_inc(s_seen0, 1)

            def statistics(src, bn_, mv_, var_, eps, steps, base):
                for a in range(2):
                    V.bn_stats(bn_[:, a, :], src(a)).then_inc(steps, 1)
                for a in range(2):
                    dve.wait_ge(steps, base + 1 + a)
                    V.bn_aggr(mv_[:, a, :], bn_[:, a, :]).then_inc(steps, 1)
                dve.wait_ge(steps, base + 4)
                V.tensor_scalar(var_[:], mv_[:, :, 1], eps, None, ALU.add).then_inc(steps, 1)

            def embedding_norms(p):
                base = LN_STEPS * p
                for a in range(2):
                    dve.wait_ge(s_emb[2 * p + a], 16)
                if p == 0:
                    dve.wait_ge(s_const, 16 * 6)
                statistics(lambda a: h[:, 2 * p + a, :], bn, mv, var_e, TOK_EPS, s_ln, base)
                for a in range(2):
                    x = h[:, 2 * p + a, :]
                    V.scalar_tensor_tensor(x, x, mv[:, a, 0:1], gam[:], ALU.subtract, ALU.mult).then_inc(s_ln, 1)
                dve.wait_ge(s_rstd, 2 * p + 1)
                for a in range(2):
                    x = h[:, 2 * p + a, :]
                    dve.wait_ge(s_ln, base + 6 + a)
                    V.scalar_tensor_tensor(x, x, rstd[:, a:a + 1], bet[:], ALU.mult, ALU.add).then_inc(s_ln, 1)
                dve.wait_ge(s_ln, base + 9)
                statistics(lambda a: h[:, 2 * p + a, :], bn, mv, var_e, LN_EPS, s_ln, base + 9)
                dve.wait_ge(s_rstd, 2 * p + 2)
                if p >= 2:
                    dve.wait_ge(s_xTp, p - 1)
                for a in range(2):
                    V.tensor_scalar(xn[:, p % 2, a, :], h[:, 2 * p + a, :], mv[:, a, 0:1], rstd[:, a:a + 1],
                                    ALU.subtract, ALU.mult).then_inc(s_xn, 1)

            cos = bc(bc(cf[:, C_COS:C_COS + HD], HEADS + KVH, 1), 2, 1)
            sin_a = bc(bc(cf[:, C_SIN:C_SIN + HD // 2], HEADS + KVH, 1), 2, 1)
            sin_b = bc(bc(cf[:, C_SIN + HD // 2:C_SIN + HD], HEADS + KVH, 1), 2, 1)
            heads = lambda ap: ap.rearrange("p a (s d) -> p a s d", d=HD)

            def rotate(p):
                dve.wait_ge(s_v, p + 1)
                base = ROPE_STEPS * p
                V.tensor_tensor(heads(qcos[:]), heads(qk_ps), cos, ALU.mult).then_inc(s_rope, 1)
                V.tensor_tensor(heads(qsin[:])[:, :, :, 0:8], heads(qk_ps)[:, :, :, 8:16], sin_a, ALU.mult).then_inc(s_rope, 1)
                V.tensor_tensor(heads(qsin[:])[:, :, :, 8:16], heads(qk_ps)[:, :, :, 0:8], sin_b, ALU.mult).then_inc(s_rope, 1)
                dve.wait_ge(s_rope, base + 3)
                V.tensor_tensor(qcos[:], qcos[:], qsin[:], ALU.add).then_inc(s_rope, 1)

            def norms(p):
                base = NORM_STEPS * p
                dve.wait_ge(s_sq, p + 1)
                V.tensor_reduce(ss[:], sq.rearrange("p a (s d) -> p (a s) d", d=HD), AX_X, ALU.add).then_inc(s_nred, 1)
                dve.wait_ge(s_nred, p + 1)
                V.tensor_scalar(ss[:], ss[:], 1e-18, None, ALU.max).then_inc(s_norm, 1)

            def stage(p):
                base = NORM_STEPS * p
                dve.wait_ge(s_root, 2 * p + 2)
                V.reciprocal(inv[:], nrm[:]).then_inc(s_norm, 1)
                dve.wait_ge(s_norm, base + 2)
                V.tensor_tensor(inv[:], inv[:], ss[:], ALU.mult).then_inc(s_norm, 1)
                dve.wait_ge(s_norm, base + 3)
                V.tensor_tensor(inv[:], inv[:], nrm[:], ALU.add).then_inc(s_norm, 1)
                dve.wait_ge(s_norm, base + 4)
                V.tensor_scalar(inv[:], inv[:], 0.5, NORM_EPS, ALU.mult, ALU.add).then_inc(s_norm, 1)
                dve.wait_ge(s_norm, base + 5)
                V.reciprocal(rn[:], inv[:]).then_inc(s_norm, 1)
                dve.wait_ge(s_norm, base + 6)
                dve.wait_ge(s_rope, ROPE_STEPS * (p + 1))
                if p >= 1:
                    dve.wait_ge(s_qhi, p)
                rn_v = bc(rn.rearrange("p (a s) -> p a s", a=2), HD, 3)
                V.tensor_tensor(q_n.rearrange("p (a s) d -> p a s d", a=2), heads(qcos[:])[:, :, 0:HEADS], rn_v[:, :, 0:HEADS],
                                ALU.mult).then_inc(s_stage, 1)
                V.tensor_tensor(k_n.rearrange("p (a s) d -> p a s d", a=2), heads(qcos[:])[:, :, HEADS:], rn_v[:, :, HEADS:],
                                ALU.mult).then_inc(s_stage, 1)
                base = STAGE_STEPS * p
                b = p % 2
                if p >= 2:
                    dve.wait_ge(s_qTp, 4 * (p - 1))
                    dve.wait_ge(s_kTp, p - 1)
                q_hi, q_lo = q_stage(b)
                q, k = bc(q_n, 2, 2), bc(k_n, 2, 2)
                kv = kst[:, b].rearrange("p a g (l c d) -> p (a g) l c d", l=2, c=2)
                dve.wait_ge(s_stage, base + 2)
                V.tensor_copy(kv[:, :, 0], k).then_inc(s_stage, 1)
                dve.wait_ge(s_stage, base + 3)
                V.tensor_tensor(kv[:, :, 1], k, kv[:, :, 0].bitcast(F32), ALU.subtract).then_inc(s_stage, 1)
                dve.wait_ge(s_qhi, p + 1)
                V.tensor_tensor(q_lo, q, q_hi.bitcast(F32), ALU.subtract).then_inc(s_stage, 1)

            def normalise_outputs(p):
                dve.wait_ge(s_ydT, 2 * (p + 1))
                V.reciprocal(rden.rearrange("p (a s) -> p a s", a=2), y_ps[:, :, :, HD]).then_inc(s_y, 1)
                dve.wait_ge(s_y, 2 * p + 1)
                if p >= 1:
                    dve.wait_ge(s_yTp, p)
                V.tensor_tensor(heads(y[:]), y_ps[:, :, :, 0:HD], bc(rden.rearrange("p (a s) -> p a s", a=2), HD, 3),
                                ALU.mult).then_inc(s_y, 1)

            def residual(p):
                dve.wait_ge(s_proj, 2 * (p + 1))
                x = h[:, 2 * p:2 * p + 2, :]
                V.tensor_tensor(x, x, ps[:, X_BANK, :].rearrange("p (a d) -> p a d", a=2), ALU.add).then_inc(s_res, 1)
                dve.wait_ge(s_res, p + 1)
                statistics(lambda a: h[:, 2 * p + a, :], bn3, mv3, var3, LN_EPS, s_ln3, 5 * p)

            def expert_input(p):
                dve.wait_ge(s_rstd3, p + 1)
                if p >= RBUF:
                    dve.wait_ge(s_scat[p % RBUF], 16 * 2 * TOPK * (p // RBUF))
                for a in range(2):
                    V.tensor_scalar(rows[:, 2 * (p % RBUF) + a, 0:D], h[:, 2 * p + a, :], mv3[:, a, 0:1], rstd3[:, a:a + 1],
                                    ALU.subtract, ALU.mult).then_inc(s_x2, 1)

            def route(p):
                base, r = ROUTE_STEPS * p, 2 * (p % RBUF)
                dve.wait_ge(s_gate, p + 1)
                V.tensor_tensor(sco[:], ps[:, QKV_BANK, 0:2 * EXPERTS].rearrange("p (a e) -> p a e", a=2),
                                bc(bg[:], 2, 1), ALU.add).then_inc(s_route, 1)
                dve.wait_ge(s_route, base + 1)
                for a in range(2):
                    V.max(top[:, 2 * p + a, :], sco[:, a, :]).then_inc(s_route, 1)
                for a in range(2):
                    dve.wait_ge(s_route, base + 2 + a)
                    V.max_index(topi[:, a, :], top[:, 2 * p + a, :], sco[:, a, :]).then_inc(s_route, 1)
                dve.wait_ge(s_route, base + 5)
                V.tensor_copy(topf[:], topi[:, :, 0:TOPK]).then_inc(s_route, 1)
                V.tensor_copy(rows[:, r:r + 2, D], cf[:, C_TOK + 2 * p:C_TOK + 2 * p + 2]).then_inc(s_route, 1)
                dve.wait_ge(s_route, base + 6)
                V.tensor_copy(rows[:, r:r + 2, D + 1], topf[:, :, 0]).then_inc(s_route, 1)
                for a in range(2):
                    V.tensor_tensor(pick[:, a], bc(cf[:, C_EID:C_EID + EXPERTS], TOPK, 1), bc(topf[:, a, :], EXPERTS, 2),
                                    ALU.is_equal).then_inc(s_route, 1)
                cbase = CHOSEN_STEPS * p
                if p == 0:
                    dve.wait_ge(s_seen0, 1)
                else:
                    dve.wait_ge(s_before, p)
                    V.tensor_tensor(seen[:, 0, :], seen[:, 1, :], chosen[:, 1, :], ALU.add).then_inc(s_seen0, 1)
                    dve.wait_ge(s_seen0, p + 1)
                dve.wait_ge(s_route, base + 10)
                V.tensor_tensor(chosen[:], pick[:, :, 0, :], pick[:, :, 1, :], ALU.add).then_inc(s_chosen, 1)
                dve.wait_ge(s_chosen, cbase + 1)
                V.tensor_tensor(seen[:, 1, :], seen[:, 0, :], chosen[:, 0, :], ALU.add).then_inc(s_chosen, 1)

            def places(p):
                dve.wait_ge(s_before, p + 1)
                V.tensor_tensor(place[:], ps[:, QKV_BANK + 1, 0:2 * EXPERTS].rearrange("p (a e) -> p a e", a=2),
                                bc(cf[:, C_ECAP:C_ECAP + EXPERTS], 2, 1), ALU.add).then_inc(s_place, 1)
                dve.wait_ge(s_place, p + 1)
                for a in range(2):
                    V.tensor_tensor(picked[:, a], pick[:, a], bc(place[:, a, :], TOPK, 1), ALU.mult).then_inc(s_picked, 1)
                dve.wait_ge(s_picked, 3 * p + 2)
                V.tensor_reduce(destf[:], picked[:], AX_X, ALU.add).then_inc(s_picked, 1)
                dve.wait_ge(s_picked, 3 * p + 3)
                V.tensor_copy(dest[:, 2 * p:2 * p + 2, :], destf[:]).then_inc(s_dest, 1)

            for i in ITERATIONS:
                if live(i - 2):
                    route(i - 2)
                if live(i - 1):
                    normalise_outputs(i - 1)
                if live(i + 1):
                    p = i + 1
                    dve.wait_ge(s_xThi, p + 1)
                    if p >= 1:
                        dve.wait_ge(s_qkv, 2 * p)
                    lo_part(xT_lo[:], X_BANK, xT_hi[:], s_xTlo)
                if live(i - 2):
                    places(i - 2)
                if live(i + 1):
                    rotate(p)
                    norms(p)
                if live(i - 1):
                    dve.wait_ge(s_yThi, i)
                    if i >= 2:
                        dve.wait_ge(s_proj, 2 * (i - 1))
                    lo_part(yT_lo[:], X_BANK, yT_hi[:], s_yTlo)
                if live(i + 1):
                    stage(p)
                if live(i + 2):
                    embedding_norms(i + 2)
                if live(i - 1):
                    residual(i - 1)
                    expert_input(i - 1)

            steps = [0]

            def table(ins):
                ins.then_inc(s_table, 1)
                steps[0] += 1
                dve.wait_ge(s_table, steps[0])

            slots = cf[:, C_SLOT:C_SLOT + SLOTS]
            dve.wait_ge(s_before_all, 1)
            table(V.tensor_copy(cnt[:], ps[:, QKV_BANK + 1, 0:EXPERTS]))
            table(V.tensor_tensor(over[:], bc(cnt[:], SEQS, 2), bc(cf[:, C_THR:C_THR + SEQS], EXPERTS, 1), ALU.is_gt))
            table(V.tensor_reduce(tiles[:], over[:], AX_X, ALU.add))
            table(V.tensor_tensor(pad_row[:], cnt[:], cf[:, C_ECAP:C_ECAP + EXPERTS], ALU.add))
            tri = cf[:, C_TRI:C_TRI + EXPERTS * EXPERTS].rearrange("p (a b) -> p a b", a=EXPERTS)
            table(V.tensor_tensor(before_e[:], bc(tiles[:], EXPERTS, 1), tri, ALU.mult))
            table(V.tensor_reduce(ends[:], before_e[:], AX_X, ALU.add))
            table(V.tensor_tensor(past[:], bc(slots, EXPERTS, 2), bc(ends[:], SLOTS, 1), ALU.is_ge))
            table(V.tensor_reduce(slot_e[:], past[:], AX_X, ALU.add))
            table(V.tensor_tensor(past_n[:], past[:], bc(tiles[:], SLOTS, 1), ALU.mult))
            table(V.tensor_reduce(slot_0[:], past_n[:], AX_X, ALU.add))
            table(V.tensor_tensor(slot_0[:], slots, slot_0[:], ALU.subtract))
            table(V.tensor_scalar(slot_r[:], slot_e[:], float(CAP), None, ALU.mult))
            table(V.scalar_tensor_tensor(slot_row[:], slot_0[:], float(P), slot_r[:], ALU.mult, ALU.add))
            table(V.tensor_scalar(slot_col[:], slot_e[:], float(EXPERTS - 1), float(D), ALU.min, ALU.mult))
            assert steps[0] == TABLE_STEPS

            def slot_lo(dst, n, hi, done):
                V.tensor_tensor(dst, ps[:, n, 0:D].rearrange("p (k t) -> p k t", k=KC), hi.bitcast(F32),
                                ALU.subtract).then_inc(done, 1)

            def column(s):
                return dve.value_load(slot_col[0:1, bass.ds(s, 1)], min_val=0, max_val=(EXPERTS - 1) * D)

            b1_f, b2_f = (raw[:, k].rearrange("p e d -> p (e d)") for k in range(2))
            dve.wait_ge(s_bias, 32)
            for s in range(-1, SLOTS + 1):
                if s + 1 < SLOTS:
                    b = (s + 1) % 2
                    dve.wait_ge(s_sxhi, s + 2)
                    if s + 1 >= 2:
                        dve.wait_ge(s_up, s)
                    slot_lo(xT_lo[:, :, b, :], b, xT_hi[:, :, b, :], s_sxlo)
                if s >= 1:
                    m = s - 1
                    dve.wait_ge(s_down, m + 1)
                    if m >= YBUF:
                        dve.wait_ge(s_sent[m % YBUF], 16 * (m // YBUF))
                    col = column(m)
                    V.tensor_tensor(slot_y[:, m % YBUF, :], ps[:, 6 + m % 2, 0:D], b2_f[:, bass.ds(col, D)],
                                    ALU.add).then_inc(s_ys, 1)
                if 0 <= s < SLOTS:
                    b = s % 2
                    dve.wait_ge(s_hThi, s + 1)
                    if s >= 2:
                        dve.wait_ge(s_down, s - 1)
                    V.scalar_tensor_tensor(yT_lo[:, :, b, :], ps[:, 4 + b, 0:D].rearrange("p (k t) -> p k t", k=KC), 0.0,
                                           yT_hi[:, :, b, :].bitcast(F32), ALU.max, ALU.subtract).then_inc(s_hTlo, 1)
                if s + 1 < SLOTS:
                    m = s + 1
                    dve.wait_ge(s_up, m + 1)
                    if m >= 2:
                        dve.wait_ge(s_hTp, m - 1)
                    col = column(m)
                    V.tensor_tensor(hid[:, m % 2, :], ps[:, 2 + m % 2, 0:D], b1_f[:, bass.ds(col, D)],
                                    ALU.add).then_inc(s_hid, 1)
                    n = m % YBUF
                    if m >= YBUF:
                        dve.wait_ge(s_sent[n], 16 * (m // YBUF))
                    V.tensor_tensor(second[:, n:n + 1], slot_x[:, m % XBUF, D + 1:D + 2], slot_e[:, bass.ds(m, 1)],
                                    ALU.not_equal).then_inc(s_isk, 1)
                    dve.wait_ge(s_isk, m + 1)
                    V.scalar_tensor_tensor(to_row[:, n:n + 1], second[:, n:n + 1], float(TOKENS),
                                           slot_x[:, m % XBUF, D:D + 1], ALU.mult, ALU.add).then_inc(s_to, 1)

            for t in range(SEQS):
                dve.wait_ge(s_back[t % CBUF], 16 * (t // CBUF + 1))
                for k in range(TOPK):
                    if k:
                        dve.wait_ge(s_mix, 2 * t + 1)
                    V.scalar_tensor_tensor(h[:, t, :], prob_c[:, t % CBUF, k, :], top[:, t, k:k + 1], h[:, t, :],
                                           ALU.mult, ALU.add).then_inc(s_mix, 1)


def constants():
    cf = np.zeros((P, C_WIDTH), np.float32)
    cf[:, C_ID:C_ID + P] = np.eye(P)
    theta = (1.0 / np.float32(10000.0) ** (np.arange(0, HD, 2, dtype=np.float32) / np.float32(HD))).astype(np.float32)
    angle = np.arange(P, dtype=np.float32)[:, None] * theta
    cf[:, C_COS:C_COS + HD] = np.tile(np.cos(angle), 2)
    cf[:, C_SIN:C_SIN + HD] = np.concatenate([-np.sin(angle), np.sin(angle)], 1)
    cf[:, C_ECAP:C_ECAP + EXPERTS] = np.arange(EXPERTS) * CAP
    cf[:, C_EID:C_EID + EXPERTS] = np.arange(EXPERTS)
    cf[:, C_SLOT:C_SLOT + SLOTS] = np.arange(SLOTS)
    cf[:, C_THR:C_THR + SEQS] = np.arange(SEQS) * P
    cf[:, C_TRI:C_TRI + EXPERTS * EXPERTS] = np.tril(np.ones((EXPERTS, EXPERTS))).ravel()
    cf[:, C_TOK:C_TOK + SEQS] = np.arange(SEQS) * P + np.arange(P)[:, None]
    cb = np.zeros((P, B_WIDTH), np.float32)
    cb[:, B_ID:B_ID + P] = np.eye(P)
    cb[:, B_BEFORE:B_BEFORE + P] = np.triu(np.ones((P, P)), 1)
    cb[:, B_ONES:B_ONES + P] = 1.0
    cb[:, B_MASK:] = np.tile(np.where(np.arange(P)[:, None] > np.arange(P), MASKED, 0.0), REP)
    return cf, cb.astype(mybir.dt.np(BF16))


def kernel(**inputs):
    import concourse.bacc as bacc
    from concourse.bass_utils import run_bass_kernel_spmd as run

    a = {k: np.asarray(v) for k, v in inputs.items()}
    wq = a["L0_attn_Wq"].reshape(KVH, REP, HD, D).transpose(1, 0, 2, 3).reshape(D, D)
    w_qkv = np.concatenate([wq, a["L0_attn_Wkv"]], 0).T
    w_proj = a["L0_attn_Wproj"].T.reshape(KVH, REP, HD, D).transpose(1, 0, 2, 3).reshape(D, D)
    cf, cb = constants()
    arrays = {
        "x_idx": a["x"].T, "seg_idx": a["mask_BS_i2_0"].T, "w_word": a["L0_tok_W_word"], "w_pos": a["L0_tok_W_pos"],
        "w_seg": a["L0_tok_W_seg"], "gamma": a["L0_tok_gamma"], "beta": a["L0_tok_beta"], "w_qkv": w_qkv,
        "w_proj": w_proj, "w_gate": a["L0_ffn_W_gate"], "b_gate": a["L0_ffn_b_gate"], "w1": a["L0_ffn_W1"],
        "b1": a["L0_ffn_b1"], "w2": a["L0_ffn_W2"], "b2": a["L0_ffn_b2"], "consts": cf, "consts_bf": cb,
    }
    arrays = {k: np.ascontiguousarray(v) for k, v in arrays.items()}
    nc = bacc.Bacc("TRN2", target_bir_lowering=False, num_devices=1)
    args = [nc.dram_tensor(k, v.shape, mybir.dt.from_np(v.dtype), kind="ExternalInput").ap() for k, v in arrays.items()]
    out = nc.dram_tensor("out", (SEQS, P, D), F32, kind="ExternalOutput").ap()
    attention_moe_program(nc, *args, out)
    result = run(nc, [arrays], core_ids=[0])
    return result.results[0]["out"]
```

```python
from contextlib import ExitStack

import numpy as np

import concourse.bass as bass
from concourse import mybir

ALU = mybir.AluOpType
ACT = mybir.ActivationFunctionType
F32 = mybir.dt.float32
F32R = mybir.dt.float32r
BF16 = mybir.dt.bfloat16
I32 = mybir.dt.int32
U32 = mybir.dt.uint32
AX_X = mybir.AxisListType.X

P = 128
SEQS = 16
PAIRS = SEQS // 2
D = 256
KC = D // P
HEADS, KVH, HD = 16, 4, 16
REP = HEADS // KVH
QK = (HEADS + KVH) * HD
QKV = QK + KVH * HD
EXPERTS, TOPK = 8, 2
TOKENS = SEQS * P
CAP = TOKENS + P
SLOTS = TOKENS * TOPK // P + EXPERTS - 1
SPARE = EXPERTS - 1
ROW = D + 2
NO_TOKEN = float(1 << 20)
LN_EPS, NORM_EPS, TOK_EPS = 1e-5, 1e-6, 1e-6
MASKED = -30000.0
PADV = 160

LN_STEPS, NORM_STEPS, ROPE_STEPS, STAGE_STEPS = 14, 6, 3, 4
ROUTE_STEPS, CHOSEN_STEPS, TABLE_STEPS = 9, 2, 12
XBUF, YBUF, CBUF, RBUF = 4, 4, 8, 2

C_ID, C_COS, C_SIN = 0, 128, 144
C_ECAP, C_EID = 160, 168
C_SLOT = 176
C_THR = C_SLOT + SLOTS
C_TRI = C_THR + SEQS
C_TOK = C_TRI + EXPERTS * EXPERTS
C_HALF = C_TOK + SEQS
C_WIDTH = C_HALF + 2
B_ID, B_BEFORE, B_ONES, B_MASK = 0, 128, 256, 384
B_WIDTH = 384 + REP * P


def attention_moe_program(nc, x_idx, seg_idx, w_word, w_pos, w_seg, gamma, beta, w_qkv, w_proj,
                          w_gate, b_gate, w1, b1, w2, b2, consts, consts_bf, out):
    x_rows = nc.dram_tensor("x_rows", (EXPERTS * CAP + SPARE * P, ROW), F32).ap()
    y_rows = nc.dram_tensor("y_rows", (TOPK * TOKENS, D), F32).ap()

    with ExitStack() as ctx:
        def sb(name, shape, dt=F32):
            return ctx.enter_context(nc.sbuf_tensor(name, shape, dt))

        def sem(name):
            return ctx.enter_context(nc.semaphore(name))

        cf = sb("cf", [P, C_WIDTH])
        cb = sb("cb", [P, B_WIDTH], BF16)
        ident = cf[:, C_ID:C_ID + P]
        gam = sb("gam", [P, D])
        bet = sb("bet", [P, D])
        bg = sb("bg", [P, EXPERTS])
        widx = sb("widx", [P, SEQS], I32)
        sidx = sb("sidx", [P, SEQS], I32)
        h = sb("h", [P, SEQS, D])
        rows = sb("rows", [P, 2 * RBUF, ROW])
        raw = sb("raw", [P, KC, EXPERTS, D])
        wq_hi = sb("wq_hi", [P, KC, QKV], F32R)
        wq_lo = sb("wq_lo", [P, KC, QKV], F32R)
        wp_hi = sb("wp_hi", [P, KC, D], F32R)
        wp_lo = sb("wp_lo", [P, KC, D], F32R)
        wg = sb("wg", [P, KC, EXPERTS])
        w1_hi = sb("w1_hi", [P, KC, EXPERTS * D], F32R)
        w1_lo = sb("w1_lo", [P, KC, EXPERTS * D], F32R)
        w2_hi = sb("w2_hi", [P, KC, EXPERTS * D], F32R)
        w2_lo = sb("w2_lo", [P, KC, EXPERTS * D], F32R)
        half = sb("half", [P, 2])

        bn = sb("bn", [P, 2, 6])
        mv = sb("mv", [P, 2, 2])
        rstd = sb("rstd", [P, 2])
        var_e = sb("var_e", [P, 2])
        xn = sb("xn", [P, 2, 2, D])
        xT_hi = sb("xT_hi", [P, KC, 2, P], F32R)
        xT_lo = sb("xT_lo", [P, KC, 2, P], F32R)
        sq = sb("sq", [P, 2, QK])
        ss = sb("ss", [P, 2 * (HEADS + KVH)])
        lnss = sb("lnss", [P, 2 * (HEADS + KVH)])
        nrm = sb("nrm", [P, 2 * (HEADS + KVH)])
        inv = sb("inv", [P, 2 * (HEADS + KVH)])
        rn = sb("rn", [P, 2 * (HEADS + KVH)])
        qcos = sb("qcos", [P, 2, QK])
        qsin = sb("qsin", [P, 2, QK])
        qst = sb("qst", [P, 2, 2, HEADS, 4 * HD], F32R)
        kst = sb("kst", [P, 2, 2, KVH, 4 * HD], F32R)
        vz = sb("vz", [P, 2, 2, KVH * PADV])
        kpad = sb("kpad", [P, 2, KVH, P], F32R)
        qT = sb("qT", [P, 2, 2, REP * P], F32R)
        prob = sb("prob", [P, 2, KVH, REP * P])
        yd = sb("yd", [P, 2, REP * P])
        rden = sb("rden", [P, 2 * HEADS])
        y = sb("y", [P, 2, D])
        yT_hi = sb("yT_hi", [P, KC, 2, P], F32R)
        yT_lo = sb("yT_lo", [P, KC, 2, P], F32R)
        x2T = sb("x2T", [P, KC, 2, P])
        sco = sb("sco", [P, 2, EXPERTS])
        top = sb("top", [P, SEQS, 8])
        topi = sb("topi", [P, 2, 8], U32)
        topf = sb("topf", [P, 2, TOPK])
        pick = sb("pick", [P, 2, TOPK, EXPERTS])
        chosen = sb("chosen", [P, 2, EXPERTS], BF16)
        seen = sb("seen", [P, 2, EXPERTS], BF16)
        place = sb("place", [P, 2, EXPERTS])
        picked = sb("picked", [P, 2, TOPK, EXPERTS])
        destf = sb("destf", [P, 2, TOPK])
        dest = sb("dest", [P, SEQS, TOPK], I32)
        pad_rows = sb("pad_rows", [P, ROW])
        bn3 = sb("bn3", [P, 2, 6])
        mv3 = sb("mv3", [P, 2, 2])
        rstd3 = sb("rstd3", [P, 2])
        var3 = sb("var3", [P, 2])
        cnt = sb("cnt", [P, EXPERTS])
        over = sb("over", [P, EXPERTS, SEQS])
        tiles = sb("tiles", [P, EXPERTS])
        before_e = sb("before_e", [P, EXPERTS, EXPERTS])
        ends = sb("ends", [P, EXPERTS])
        slot_e = sb("slot_e", [P, SLOTS])
        slot_0 = sb("slot_0", [P, SLOTS])
        slot_r = sb("slot_r", [P, SLOTS])
        slot_row = sb("slot_row", [P, SLOTS], I32)
        slot_col = sb("slot_col", [P, SLOTS], I32)
        pad_row = sb("pad_row", [P, EXPERTS], I32)
        second = sb("second", [P, YBUF])
        to_row = sb("to_row", [P, YBUF], I32)

        ps = ctx.enter_context(nc.psum_tensor("ps", [P, 8, 512], F32))

        s_const = sem("s_const")
        s_idx = sem("s_idx")
        s_pos = [sem(f"s_pos{n}") for n in range(5)]
        s_word = [sem(f"s_word{t}") for t in range(SEQS)]
        s_emb = [sem(f"s_emb{t}") for t in range(SEQS)]
        s_wraw = sem("s_wraw")
        s_w1raw, s_w2raw = sem("s_w1raw"), sem("s_w2raw")
        s_hi, s_split_hi, s_split = sem("s_hi"), sem("s_split_hi"), sem("s_split")
        s_half, s_seen0, s_nred, s_root = sem("s_half"), sem("s_seen0"), sem("s_nred"), sem("s_root")
        s_qhi = sem("s_qhi")
        s_place, s_picked, s_rstd3 = sem("s_place"), sem("s_picked"), sem("s_rstd3")
        s_init = sem("s_init")
        s_ln = sem("s_ln")
        s_rstd = sem("s_rstd")
        s_xn = sem("s_xn")
        s_xTp, s_xThi, s_xTlo = sem("s_xTp"), sem("s_xThi"), sem("s_xTlo")
        s_qkv = sem("s_qkv")
        s_sq, s_rope, s_norm, s_v = sem("s_sq"), sem("s_rope"), sem("s_norm"), sem("s_v")
        s_stage = sem("s_stage")
        s_kTp, s_kT = sem("s_kTp"), sem("s_kT")
        s_qTp, s_qT = sem("s_qTp"), sem("s_qT")
        s_score, s_prob = sem("s_score"), sem("s_prob")
        s_pv, s_yd = sem("s_pv"), sem("s_yd")
        s_ydT, s_y = sem("s_ydT"), sem("s_y")
        s_yTp, s_yThi, s_yTlo = sem("s_yTp"), sem("s_yThi"), sem("s_yTlo")
        s_proj, s_res = sem("s_proj"), sem("s_res")
        s_ln3, s_x2 = sem("s_ln3"), sem("s_x2")
        s_x2Tp, s_x2T = sem("s_x2Tp"), sem("s_x2T")
        s_gate, s_route, s_chosen, s_before, s_dest = (sem("s_gate"), sem("s_route"), sem("s_chosen"),
                                                       sem("s_before"), sem("s_dest"))
        s_scat = [sem(f"s_scat{n}") for n in range(RBUF)]
        s_before_all, s_table = sem("s_before_all"), sem("s_table")
        s_pads, s_pool_pads = sem("s_pads"), sem("s_pool_pads")
        s_bias, s_padrow, s_add = sem("s_bias"), sem("s_padrow"), sem("s_add")
        s_qlo, s_cnt = sem("s_qlo"), sem("s_cnt")
        s_slot = [sem(f"s_slot{n}") for n in range(XBUF)]
        s_sxp, s_sxhi, s_sxlo = sem("s_sxp"), sem("s_sxhi"), sem("s_sxlo")
        s_up, s_hid = sem("s_up"), sem("s_hid")
        s_hTp, s_hThi, s_hTlo = sem("s_hTp"), sem("s_hThi"), sem("s_hTlo")
        s_down, s_ys = sem("s_down"), sem("s_ys")
        s_isk, s_to = sem("s_isk"), sem("s_to")
        s_sent = [sem(f"s_sent{n}") for n in range(YBUF)]
        s_back = [sem(f"s_back{n}") for n in range(CBUF)]
        s_mix, s_out = sem("s_mix"), sem("s_out")

        def bc(ap, n, axis):
            ap = ap.unsqueeze(axis)
            shape = list(ap.shape)
            shape[axis] = n
            return ap.broadcast_to(shape)

        def part(t, *shape):
            flat = t.rearrange("p a c -> p (a c)") if len(t.shape) == 3 else t.rearrange("p b a c -> p (b a c)")
            return flat[:, 0:shape[0] * shape[1]].rearrange("p (m n) -> p m n", m=shape[0])

        past, past_n = part(qcos, SLOTS, EXPERTS), part(qsin, SLOTS, EXPERTS)
        slot_x, slot_y, hid = part(vz, XBUF, ROW), part(yd, YBUF, D), y
        prob_f = prob.rearrange("p a g n -> p (a g n)")
        b1_f, b2_f = prob_f[:, 0:EXPERTS * D], prob_f[:, EXPERTS * D:2 * EXPERTS * D]
        coming = raw.rearrange("p k e d -> p (k e d)").rearrange("p (c k d) -> p c k d", c=CBUF, k=TOPK)
        POS = [(0, 2), (2, 4), (4, 8), (8, 12), (12, SEQS)]
        def bank(n, cols=512):
            return ps[:, n, 0:cols]

        S_BANK, Q_BANK, X_BANK, V_BANK, QKV_BANK = 0, 2, 4, 5, 6
        qk_ps = ps[:, QKV_BANK:QKV_BANK + 2, 0:QK]
        v_ps = ps[:, QKV_BANK:QKV_BANK + 2, QK:QKV].rearrange("p a (g d) -> p a g d", d=HD)
        y_ps = ps[:, Q_BANK:Q_BANK + 2, :].rearrange("p a (s c) -> p a s c", c=2 * HD)
        vz_v = vz.rearrange("p b a (g c) -> p b a g c", c=PADV)
        qk_n = qsin.rearrange("p a n -> p (a n)")
        q_n = qk_n[:, 0:2 * HEADS * HD].rearrange("p (s d) -> p s d", d=HD)
        k_n = qk_n[:, 2 * HEADS * HD:].rearrange("p (s d) -> p s d", d=HD)

        def q_stage(b):
            v = qst[:, b].rearrange("p a s (c l d) -> p (a s) c l d", c=2, l=2)
            return v[:, :, :, 0], v[:, :, :, 1]

        raw_f = raw.rearrange("p k e d -> p (k e d)")
        w1_f = [w1_hi.rearrange("p k n -> p (k n)"), w1_lo.rearrange("p k n -> p (k n)")]
        w2_f = [w2_hi.rearrange("p k n -> p (k n)"), w2_lo.rearrange("p k n -> p (k n)")]
        PIECES = 4
        PIECE = KC * EXPERTS * D // PIECES
        ITERATIONS = range(-2, PAIRS + 2)

        def live(p):
            return 0 <= p < PAIRS

        def write_padding(eng, first, end, done):
            eng.wait_ge(s_padrow, 1)
            for e in range(first, end):
                at = eng.value_load(pad_row[0:1, e:e + 1], min_val=e * CAP, max_val=e * CAP + TOKENS)
                eng.dma_start(x_rows[bass.ds(at, P), :], pad_rows[:]).then_inc(done, 16)

        block = ctx.enter_context(nc.Block())

        @block.sync
        def _(sp):
            sp.dma_start(widx[:], x_idx).then_inc(s_idx, 16)
            sp.dma_start(sidx[:], seg_idx).then_inc(s_idx, 16)
            for n, (a, b) in enumerate(POS):
                if n == 1:
                    sp.dma_start(gam[:], gamma.partition_broadcast(P)).then_inc(s_const, 16)
                    sp.dma_start(bet[:], beta.partition_broadcast(P)).then_inc(s_const, 16)
                    sp.dma_start(cf[:], consts).then_inc(s_const, 16)
                    sp.dma_start(cb[:], consts_bf).then_inc(s_const, 16)
                    sp.dma_start(bg[:], b_gate.partition_broadcast(P)).then_inc(s_const, 16)
                    sp.dma_start(wg[:], w_gate.rearrange("(k p) e -> p k e", p=P)).then_inc(s_const, 16)
                    sp.wait_ge(s_emb[1], 16)
                sp.dma_start(h[:, a:b, :], bc(w_pos, b - a, 1)).then_inc(s_pos[n], 16)
            sp.wait_ge(s_hi, 4)
            for k in range(KC):
                sp.dma_start(raw[:, k], w1.rearrange("e (k p) d -> k p e d", p=P)[k]).then_inc(s_w1raw, 16)
            sp.wait_ge(s_split, 8)
            for k in range(KC):
                sp.dma_start(raw[:, k], w2.rearrange("e (k p) d -> k p e d", p=P)[k]).then_inc(s_w2raw, 16)
            sp.wait_ge(s_pv, 2 * PAIRS)
            sp.dma_start(b1_f, b1.rearrange("e d -> (e d)").partition_broadcast(P)).then_inc(s_bias, 16)
            sp.dma_start(b2_f, b2.rearrange("e d -> (e d)").partition_broadcast(P)).then_inc(s_bias, 16)
            write_padding(sp, 0, 3, s_pads)
            sp.wait_ge(s_pads, 16 * (6 + SPARE))
            sp.wait_ge(s_pool_pads, 16 * 2)
            for n in range(RBUF):
                sp.wait_ge(s_scat[n], 16 * 2 * TOPK * (PAIRS // RBUF))
            sp.wait_ge(s_table, TABLE_STEPS)

            def load_slot(s, n):
                row = sp.value_load(slot_row[0:1, bass.ds(s, 1)], min_val=0, max_val=EXPERTS * CAP + (SPARE - 1) * P)
                sp.dma_start(slot_x[:, n, :], x_rows[bass.ds(row, P), :]).then_inc(s_slot[n], 16)

            for s in range(XBUF):
                load_slot(s, s)
            for s in range(XBUF, SLOTS):
                sp.wait_ge(s_sxp, s - XBUF + 1)
                sp.wait_ge(s_to, s - XBUF + 1)
                load_slot(s, s % XBUF)

            for n in range(YBUF):
                sp.wait_ge(s_sent[n], 16 * len(range(n, SLOTS, YBUF)))
            back = y_rows.rearrange("(k t p) d -> t p k d", k=TOPK, p=P)
            for t in range(SEQS):
                n = t % CBUF
                if t >= CBUF:
                    sp.wait_ge(s_mix, 2 * (t - CBUF + 2 - t % 2))
                sp.dma_start(coming[:, n], back[t]).then_inc(s_back[n], 16)

        @block.gpsimd
        def _(pool):
            def gather(t, table, idx, done):
                nc.gpsimd.indirect_dma_start(
                    out=h[:, t, :], out_offset=None, in_=table,
                    in_offset=bass.IndirectOffsetOnAxis(ap=idx[:, t:t + 1], axis=0),
                    compute_op=ALU.add).then_inc(done, 16)

            def words(t):
                pool.wait_ge(s_pos[max(n for n, (a, b) in enumerate(POS) if a <= t)], 16)
                gather(t, w_word, widx, s_word[t])

            def segments(t):
                pool.wait_ge(s_word[t], 16)
                gather(t, w_seg, sidx, s_emb[t])

            pool.wait_ge(s_idx, 32)
            for t in range(2):
                words(t)
            nc.gpsimd.memset(half[:], -0.5).then_inc(s_half, 1)
            nc.gpsimd.memset(pad_rows[:, 0:D], 0.0).then_inc(s_half, 1)
            nc.gpsimd.memset(pad_rows[:, D:D + 1], NO_TOKEN).then_inc(s_half, 1)
            nc.gpsimd.memset(pad_rows[:, D + 1:ROW], 0.0).then_inc(s_half, 1)
            for t in range(2):
                segments(t)
            nc.gpsimd.memset(kpad[:].bitcast(F32), 0.0).then_inc(s_init, 1)
            nc.gpsimd.memset(vz[:], 0.0).then_inc(s_half, 1)
            pool.wait_ge(s_half, 5)
            nc.gpsimd.memset(vz_v[:, :, :, :, HD:HD + 1], 1.0).then_inc(s_init, 1)

            def power(out_ap, in_ap, done):
                nc.gpsimd.tensor_tensor(out_ap, in_ap, half[:, 0:2], ALU.pow).then_inc(done, 1)

            for i in ITERATIONS:
                if live(i - 2):
                    pool.wait_ge(s_ln3, 5 * (i - 1))
                    power(rstd3[:], var3[:], s_rstd3)
                for t in (2 * (i + 3), 2 * (i + 3) + 1):
                    if t < SEQS:
                        words(t)
                if live(i + 2):
                    p = i + 2
                    pool.wait_ge(s_ln, LN_STEPS * p + 5)
                    power(rstd[:], var_e[:], s_rstd)
                if live(i + 1):
                    pool.wait_ge(s_rope, ROPE_STEPS * (i + 2))
                    nc.gpsimd.tensor_tensor(qcos[:], qcos[:], qsin[:], ALU.add).then_inc(s_add, 1)
                if live(i + 2):
                    pool.wait_ge(s_ln, LN_STEPS * p + 14)
                    power(rstd[:], var_e[:], s_rstd)
                for t in (2 * (i + 3), 2 * (i + 3) + 1):
                    if t < SEQS:
                        segments(t)
                if live(i + 1):
                    p = i + 1
                    q_hi, q_lo = q_stage(p % 2)
                    pool.wait_ge(s_qhi, p + 1)
                    nc.gpsimd.tensor_tensor(q_lo, bc(q_n, 2, 2), q_hi.bitcast(F32), ALU.subtract).then_inc(s_qlo, 1)
                if live(i - 2):
                    p = i - 2
                    pool.wait_ge(s_dest, p + 1)
                    for t in (2 * p, 2 * p + 1):
                        for k in range(TOPK):
                            nc.gpsimd.indirect_dma_start(
                                out=x_rows, out_offset=bass.IndirectOffsetOnAxis(ap=dest[:, t, k:k + 1], axis=0),
                                in_=rows[:, t % (2 * RBUF), :], in_offset=None).then_inc(s_scat[p % RBUF], 16)

            write_padding(nc.gpsimd, 3, 5, s_pool_pads)

            def send(s, n):
                nc.gpsimd.indirect_dma_start(
                    out=y_rows, out_offset=bass.IndirectOffsetOnAxis(ap=to_row[:, n:n + 1], axis=0),
                    in_=slot_y[:, n, :], in_offset=None, bounds_check=TOPK * TOKENS - 1,
                    oob_is_err=False).then_inc(s_sent[n], 16)

            for s in range(SLOTS):
                pool.wait_ge(s_ys, s + 1)
                pool.wait_ge(s_to, s + 1)
                send(s, s % YBUF)

        @block.tensor
        def _(pe):
            def split_product(out_ap, lhs, rhs, start=True, stop=True):
                n = len(lhs)
                for k in range(n):
                    (ah, al), (bh, bl) = lhs[k], rhs[k]
                    nc.tensor.matmul(out_ap, ah, bh, start=start and k == 0, stop=False)
                    nc.tensor.matmul(out_ap, ah, bl, start=False, stop=False)
                    last = nc.tensor.matmul(out_ap, al, bh, start=False, stop=stop and k == n - 1)
                return last

            def transpose_pair(n, src, done):
                for k in range(KC):
                    for a in range(2):
                        c = (2 * k + a) * P
                        last = nc.tensor.transpose(ps[:, n, c:c + P], src(a)[:, k * P:(k + 1) * P], ident)
                last.then_inc(done, 1)

            def q_transposes(p, a):
                for pr in range(2):
                    m = 4 * p + 2 * a + pr
                    if pr == 0:
                        pe.wait_ge(s_qlo, p + 1)
                    if m >= 2:
                        pe.wait_ge(s_qT, m - 1)
                    for j in range(REP):
                        two = qst[:, p % 2, a, 4 * j + 2 * pr:4 * j + 2 * pr + 2, :].rearrange("p s c -> p (s c)")
                        last = nc.tensor.transpose(ps[:, Q_BANK + pr, j * P:(j + 1) * P], two.bitcast(F32), ident)
                    last.then_inc(s_qTp, 1)

            def k_transposes(p):
                pe.wait_ge(s_stage, STAGE_STEPS * (p + 1))
                if p >= 1:
                    pe.wait_ge(s_yd, 2 * p)
                for a in range(2):
                    for pr in range(2):
                        c = (2 * a + pr) * P
                        keys = kst[:, p % 2, a, 2 * pr:2 * pr + 2, :].rearrange("p g c -> p (g c)").bitcast(F32)
                        last = nc.tensor.transpose(ps[:, V_BANK, c:c + P], keys, ident)
                last.then_inc(s_kTp, 1)

            def scores(p, a):
                for g in range(KVH):
                    m = 8 * p + 4 * a + g
                    if g == 0:
                        pe.wait_ge(s_kT, 2 * (p + 1))
                        pe.wait_ge(s_const, 16 * 6)
                    pe.wait_ge(s_qT, 4 * p + 2 * a + g // 2 + 1)
                    if m >= 2:
                        pe.wait_ge(s_prob, m - 1)
                    o = bank(S_BANK + g % 2)
                    nc.tensor.matmul(o, kpad[:, a, g, :], qT[:, a, g // 2, :], start=True, stop=False)
                    nc.tensor.matmul(o, cb[:, B_ID:B_ID + P], cb[:, B_MASK:B_MASK + REP * P],
                                     start=False, stop=True).then_inc(s_score, 1)

            def values(p, a):
                if a == 0:
                    pe.wait_ge(s_kT, 2 * (p + 1))
                    pe.wait_ge(s_v, p + 1)
                    pe.wait_ge(s_init, 2)
                else:
                    pe.wait_ge(s_yd, 2 * p + 1)
                for g in range(KVH):
                    pe.wait_ge(s_prob, 8 * p + 4 * a + g + 1)
                    last = nc.tensor.matmul(bank(V_BANK), vz[:, p % 2, a, g * P:(g + 1) * P], prob[:, a, g, :],
                                            start=(g == 0), stop=(g == KVH - 1))
                last.then_inc(s_pv, 1)

            def gate(p):
                pe.wait_ge(s_x2T, p + 1)
                for a in range(2):
                    for k in range(KC):
                        last = nc.tensor.matmul(ps[:, X_BANK, EXPERTS * a:EXPERTS * (a + 1)], x2T[:, k, a, :],
                                                wg[:, k, :], start=(k == 0), stop=(k == KC - 1))
                last.then_inc(s_gate, 1)

            def before(p):
                pe.wait_ge(s_chosen, CHOSEN_STEPS * (p + 1))
                o = ps[:, X_BANK, 0:2 * EXPERTS]
                nc.tensor.matmul(o, cb[:, B_BEFORE:B_BEFORE + P], chosen.rearrange("p a e -> p (a e)"),
                                 start=True, stop=False)
                nc.tensor.matmul(o, cb[:, B_ONES:B_ONES + P], seen.rearrange("p a e -> p (a e)"),
                                 start=False, stop=True).then_inc(s_before, 1)

            def output_transposes(p):
                for a in range(2):
                    pe.wait_ge(s_yd, 2 * p + a + 1)
                    if a == 0:
                        pe.wait_ge(s_qT, 4 * p + 6 if live(p + 1) else 4 * p + 4)
                    for j in range(REP):
                        last = nc.tensor.transpose(ps[:, Q_BANK + a, j * P:(j + 1) * P],
                                                   yd[:, a, j * P:(j + 1) * P], ident)
                    last.then_inc(s_ydT, 1)

            pe.wait_ge(s_const, 16 * 6)
            for i in ITERATIONS:
                if live(i + 1):
                    pe.wait_ge(s_xn, 2 * (i + 2))
                    if live(i - 2):
                        pe.wait_ge(s_res, i - 1)
                    transpose_pair(X_BANK, lambda a: xn[:, (i + 1) % 2, a, :], s_xTp)
                if live(i):
                    k_transposes(i)
                    q_transposes(i, 0)
                if live(i + 1):
                    pe.wait_ge(s_xTlo, i + 2)
                    pe.wait_ge(s_xThi, i + 2)
                    if i == -1:
                        pe.wait_ge(s_hi, 4)
                    if live(i):
                        pe.wait_ge(s_v, i + 1)
                        pe.wait_ge(s_rope, ROPE_STEPS * (i + 1))
                    for a in range(2):
                        last = split_product(ps[:, QKV_BANK + a, 0:QKV],
                                             [(xT_hi[:, k, a, :], xT_lo[:, k, a, :]) for k in range(KC)],
                                             [(wq_hi[:, k, :], wq_lo[:, k, :]) for k in range(KC)])
                        last.then_inc(s_qkv, 1)
                if live(i):
                    scores(i, 0)
                if live(i - 1):
                    output_transposes(i - 1)
                if live(i - 2):
                    pe.wait_ge(s_x2, 2 * (i - 1))
                    transpose_pair(X_BANK, lambda a: rows[:, 2 * ((i - 2) % RBUF) + a, 0:D], s_x2Tp)
                    gate(i - 2)
                if live(i):
                    values(i, 0)
                if live(i - 2):
                    before(i - 2)
                if live(i):
                    if i >= 1:
                        pe.wait_ge(s_y, 2 * i)
                    q_transposes(i, 1)
                    scores(i, 1)
                if live(i - 1):
                    pe.wait_ge(s_y, 2 * i)
                    if live(i - 2):
                        pe.wait_ge(s_place, i - 1)
                    transpose_pair(X_BANK, lambda a: y[:, a, :], s_yTp)
                if live(i):
                    values(i, 1)
                if live(i - 1):
                    pe.wait_ge(s_yTlo, i)
                    pe.wait_ge(s_yThi, i)
                    for a in range(2):
                        last = split_product(ps[:, X_BANK, a * D:(a + 1) * D],
                                             [(yT_hi[:, k, a, :], yT_lo[:, k, a, :]) for k in range(KC)],
                                             [(wp_hi[:, k, :], wp_lo[:, k, :]) for k in range(KC)])
                        last.then_inc(s_proj, 1)

            pe.wait_ge(s_place, PAIRS)
            nc.tensor.matmul(ps[:, X_BANK, 0:EXPERTS], cb[:, B_ONES:B_ONES + P], seen[:, 1, :],
                             start=True, stop=False)
            nc.tensor.matmul(ps[:, X_BANK, 0:EXPERTS], cb[:, B_ONES:B_ONES + P], chosen[:, 1, :],
                             start=False, stop=True).then_inc(s_before_all, 1)

            SX, SH, ST, SY = 0, 2, 4, 6

            def slot_transposes(s, b, n):
                pe.wait_ge(s_slot[n], (s // XBUF + 1) * 16)
                if s >= 2:
                    pe.wait_ge(s_sxhi, s - 1)
                    pe.wait_ge(s_sxlo, s - 1)
                for k in range(KC):
                    last = nc.tensor.transpose(ps[:, SX + b, k * P:(k + 1) * P], slot_x[:, n, k * P:(k + 1) * P], ident)
                last.then_inc(s_sxp, 1)

            def up(s, b, col):
                pe.wait_ge(s_sxhi, s + 1)
                pe.wait_ge(s_sxlo, s + 1)
                if s >= 2:
                    pe.wait_ge(s_hid, s - 1)
                split_product(ps[:, SH + b, 0:D], [(xT_hi[:, k, b, :], xT_lo[:, k, b, :]) for k in range(KC)],
                              [(w1_hi[:, k, bass.ds(col, D)], w1_lo[:, k, bass.ds(col, D)]) for k in range(KC)]
                              ).then_inc(s_up, 1)

            def hidden_transposes(s, b):
                pe.wait_ge(s_hid, s + 1)
                if s >= 2:
                    pe.wait_ge(s_hThi, s - 1)
                    pe.wait_ge(s_hTlo, s - 1)
                for k in range(KC):
                    last = nc.tensor.transpose(ps[:, ST + b, k * P:(k + 1) * P], hid[:, b, k * P:(k + 1) * P], ident)
                last.then_inc(s_hTp, 1)

            def down(s, b, col):
                pe.wait_ge(s_hThi, s + 1)
                pe.wait_ge(s_hTlo, s + 1)
                if s >= 2:
                    pe.wait_ge(s_ys, s - 1)
                split_product(ps[:, SY + b, 0:D], [(yT_hi[:, k, b, :], yT_lo[:, k, b, :]) for k in range(KC)],
                              [(w2_hi[:, k, bass.ds(col, D)], w2_lo[:, k, bass.ds(col, D)]) for k in range(KC)]
                              ).then_inc(s_down, 1)

            def column(s):
                return pe.value_load(slot_col[0:1, bass.ds(s, 1)], min_val=0, max_val=(EXPERTS - 1) * D)

            pe.wait_ge(s_table, TABLE_STEPS)
            pe.wait_ge(s_split, 16)
            for s in range(-2, SLOTS + 1):
                if s + 2 < SLOTS:
                    slot_transposes(s + 2, s % 2, (s + 2) % XBUF)
                if 0 <= s + 1 < SLOTS:
                    up(s + 1, (s + 1) % 2, column(s + 1))
                if 0 <= s < SLOTS:
                    hidden_transposes(s, s % 2)
                if s >= 1:
                    down(s - 1, (s - 1) % 2, column(s - 1))

        @block.scalar
        def _(act):
            act.dma_start(raw_f[:, 0:KC * QKV].rearrange("p (k n) -> p k n", k=KC),
                          w_qkv.rearrange("(k p) n -> p k n", p=P)).then_inc(s_wraw, 16)
            act.dma_start(raw_f[:, KC * QKV:KC * (QKV + D)].rearrange("p (k n) -> p k n", k=KC),
                          w_proj.rearrange("(k p) n -> p k n", p=P)).then_inc(s_wraw, 16)
            def copy(out_ap, in_ap, done):
                nc.scalar.activation(out_ap, in_ap, ACT.Copy).then_inc(done, 1)

            def x_bank(n=X_BANK):
                return ps[:, n, :].rearrange("p (k a t) -> p k a t", k=KC, a=2)

            def q_copies(p, a):
                for pr in range(2):
                    m = 4 * p + 2 * a + pr
                    act.wait_ge(s_qTp, m + 1)
                    if p >= 1:
                        act.wait_ge(s_score, 8 * (p - 1) + 4 * a + 2 * pr + 2)
                    copy(qT[:, a, pr, :], bank(Q_BANK + pr), s_qT)

            def probabilities(p, a, groups):
                for g in groups:
                    m = 8 * p + 4 * a + g
                    act.wait_ge(s_score, m + 1)
                    if p >= 1 and g == 0:
                        act.wait_ge(s_pv, 2 * (p - 1) + a + 1)
                    nc.scalar.activation(prob[:, a, g, :], bank(S_BANK + g % 2), ACT.Exp,
                                         scale=float(HD) ** -0.5).then_inc(s_prob, 1)

            def outputs(p, a):
                act.wait_ge(s_pv, 2 * p + a + 1)
                if p >= 1:
                    act.wait_ge(s_ydT, 2 * (p - 1) + a + 1)
                copy(yd[:, a, :], bank(V_BANK), s_yd)

            act.preload_act_table_set("natural_log_exp_and_others")
            act.wait_ge(s_w1raw, 16 * KC)
            for c in range(PIECES):
                copy(w1_f[0][:, c * PIECE:(c + 1) * PIECE], raw_f[:, c * PIECE:(c + 1) * PIECE], s_split_hi)
            act.wait_ge(s_half, 4)
            for n in range(SPARE):
                act.dma_start(x_rows[EXPERTS * CAP + n * P:EXPERTS * CAP + (n + 1) * P, :],
                              pad_rows[:]).then_inc(s_pads, 16)

            def attention_input(p):
                act.wait_ge(s_xTp, p + 1)
                if p >= 1:
                    act.wait_ge(s_qkv, 2 * p)
                    act.wait_ge(s_xTlo, p)
                copy(xT_hi[:], x_bank(), s_xThi)

            def keys(p):
                act.wait_ge(s_kTp, p + 1)
                if p == 0:
                    act.wait_ge(s_init, 2)
                else:
                    act.wait_ge(s_score, 8 * p)
                kT = bank(V_BANK).rearrange("p (a r t) -> p a r t", a=2, r=2)
                kp = kpad.rearrange("p a (r o) t -> p a r o t", o=2)
                copy(kp[0:64, :, :, 0, :], kT[0:64], s_kT)
                copy(kp[64:128, :, :, 1, :], kT[64:128], s_kT)

            def squares_and_values(p):
                act.wait_ge(s_qkv, 2 * (p + 1))
                if p >= 1:
                    act.wait_ge(s_nred, p)
                nc.scalar.activation(sq[:], qk_ps, ACT.Square).then_inc(s_sq, 1)
                if p >= 2:
                    act.wait_ge(s_pv, 2 * (p - 1))
                if p == 0:
                    act.wait_ge(s_init, 2)
                copy(vz_v[:, p % 2, :, :, 0:HD], v_ps, s_v)

            def roots(p):
                act.wait_ge(s_norm, NORM_STEPS * p + 1)
                nc.scalar.activation(lnss[:], ss[:], ACT.Ln).then_inc(s_root, 1)
                act.wait_ge(s_root, 2 * p + 1)
                nc.scalar.activation(nrm[:], lnss[:], ACT.Exp, scale=0.5).then_inc(s_root, 1)

            for i in ITERATIONS:
                if live(i + 1):
                    attention_input(i + 1)
                if live(i):
                    keys(i)
                    q_copies(i, 0)
                if live(i + 1):
                    squares_and_values(i + 1)
                if live(i):
                    probabilities(i, 0, range(0, 2))
                if live(i + 1):
                    roots(i + 1)
                if live(i):
                    probabilities(i, 0, range(2, KVH))
                if live(i - 2):
                    act.wait_ge(s_x2Tp, i - 1)
                    if i >= 3:
                        act.wait_ge(s_gate, i - 2)
                    copy(x2T[:], x_bank(), s_x2T)
                if live(i):
                    outputs(i, 0)
                    q_copies(i, 1)
                    probabilities(i, 1, range(0, KVH))
                if live(i + 1):
                    act.wait_ge(s_stage, STAGE_STEPS * (i + 1) + 2)
                    if i >= 1:
                        act.wait_ge(s_qTp, 4 * i)
                    copy(q_stage((i + 1) % 2)[0], bc(q_n, 2, 2), s_qhi)
                if live(i - 1):
                    act.wait_ge(s_yTp, i)
                    if i >= 2:
                        act.wait_ge(s_proj, 2 * (i - 1))
                        act.wait_ge(s_yTlo, i - 1)
                    copy(yT_hi[:], x_bank(), s_yThi)
                if live(i):
                    outputs(i, 1)
                if i == PAIRS:
                    act.wait_ge(s_w2raw, 16 * KC)
                    for c in range(PIECES):
                        copy(w2_f[0][:, c * PIECE:(c + 1) * PIECE], raw_f[:, c * PIECE:(c + 1) * PIECE], s_split_hi)
            write_padding(act, 5, EXPERTS, s_pads)

            def slot_copy(dst, n, done):
                copy(dst, ps[:, n, 0:D].rearrange("p (k t) -> p k t", k=KC), done)

            for s in range(-2, SLOTS):
                if s + 2 < SLOTS:
                    m = s + 2
                    act.wait_ge(s_sxp, m + 1)
                    if m >= 2:
                        act.wait_ge(s_up, m - 1)
                        act.wait_ge(s_sxlo, m - 1)
                    slot_copy(xT_hi[:, :, m % 2, :], m % 2, s_sxhi)
                if s >= 0:
                    b = s % 2
                    act.wait_ge(s_hTp, s + 1)
                    if s >= 2:
                        act.wait_ge(s_down, s - 1)
                        act.wait_ge(s_hTlo, s - 1)
                    nc.scalar.activation(yT_hi[:, :, b, :], ps[:, 4 + b, 0:D].rearrange("p (k t) -> p k t", k=KC),
                                         ACT.Relu).then_inc(s_hThi, 1)
            for t in range(0, SEQS, 2):
                act.wait_ge(s_mix, 2 * (t + 2))
                act.dma_start(out.rearrange("t p d -> p t d")[:, t:t + 2], h[:, t:t + 2, :]).then_inc(s_out, 16)
            act.wait_ge(s_out, 16 * PAIRS)

        @block.vector
        def _(dve):
            V = nc.vector

            def lo_part(dst, n, hi, done):
                V.tensor_tensor(dst, ps[:, n, :].rearrange("p (k a t) -> p k a t", k=KC, a=2), hi.bitcast(F32),
                                ALU.subtract).then_inc(done, 1)

            dve.wait_ge(s_wraw, 32)
            for n, (hi, lo, a, b) in enumerate(((wq_hi, wq_lo, 0, KC * QKV), (wp_hi, wp_lo, KC * QKV, KC * (QKV + D)))):
                V.tensor_copy(hi.rearrange("p k n -> p (k n)"), raw_f[:, a:b]).then_inc(s_hi, 1)
                dve.wait_ge(s_hi, 2 * n + 1)
                V.tensor_tensor(lo.rearrange("p k n -> p (k n)"), raw_f[:, a:b],
                                hi.rearrange("p k n -> p (k n)").bitcast(F32), ALU.subtract).then_inc(s_hi, 1)
            V.memset(seen[:], 0.0).then_inc(s_seen0, 1)

            def low_weights(parts, c, high):
                a, b = c * PIECE, (c + 1) * PIECE
                dve.wait_ge(s_split_hi, high)
                V.tensor_tensor(parts[1][:, a:b], raw_f[:, a:b], parts[0][:, a:b].bitcast(F32), ALU.subtract).then_inc(s_split, 2)

            def statistics(src, bn_, mv_, var_, eps, steps, base):
                for a in range(2):
                    V.bn_stats(bn_[:, a, :], src(a)).then_inc(steps, 1)
                for a in range(2):
                    dve.wait_ge(steps, base + 1 + a)
                    V.bn_aggr(mv_[:, a, :], bn_[:, a, :]).then_inc(steps, 1)
                dve.wait_ge(steps, base + 4)
                V.tensor_scalar(var_[:], mv_[:, :, 1], eps, None, ALU.add).then_inc(steps, 1)

            def embedding_norms(p, step):
                base = LN_STEPS * p
                pair = h[:, 2 * p:2 * p + 2, :]
                if step == 0:
                    for a in range(2):
                        dve.wait_ge(s_emb[2 * p + a], 16)
                    statistics(lambda a: pair[:, a, :], bn, mv, var_e, TOK_EPS, s_ln, base)
                if step == 1:
                    if p == 0:
                        dve.wait_ge(s_const, 16 * 6)
                    for a in range(2):
                        V.scalar_tensor_tensor(pair[:, a, :], pair[:, a, :], mv[:, a, 0:1], gam[:], ALU.subtract,
                                               ALU.mult).then_inc(s_ln, 1)
                if step in (2, 3):
                    a = step - 2
                    dve.wait_ge(s_rstd, 2 * p + 1)
                    dve.wait_ge(s_ln, base + 6 + a)
                    V.scalar_tensor_tensor(pair[:, a, :], pair[:, a, :], rstd[:, a:a + 1], bet[:], ALU.mult,
                                           ALU.add).then_inc(s_ln, 1)
                if step in (4, 5):
                    a = step - 4
                    dve.wait_ge(s_ln, base + 8 + a)
                    V.bn_stats(bn[:, a, :], pair[:, a, :]).then_inc(s_ln, 1)
                if step == 6:
                    for a in range(2):
                        dve.wait_ge(s_ln, base + 10 + a)
                        V.bn_aggr(mv[:, a, :], bn[:, a, :]).then_inc(s_ln, 1)
                    dve.wait_ge(s_ln, base + 13)
                    V.tensor_scalar(var_e[:], mv[:, :, 1], LN_EPS, None, ALU.add).then_inc(s_ln, 1)
                if step == 7:
                    dve.wait_ge(s_rstd, 2 * p + 2)
                    if p >= 2:
                        dve.wait_ge(s_xTp, p - 1)
                    for a in range(2):
                        V.tensor_scalar(xn[:, p % 2, a, :], pair[:, a, :], mv[:, a, 0:1], rstd[:, a:a + 1],
                                        ALU.subtract, ALU.mult).then_inc(s_xn, 1)

            cos = bc(bc(cf[:, C_COS:C_COS + HD], HEADS + KVH, 1), 2, 1)
            sin_a = bc(bc(cf[:, C_SIN:C_SIN + HD // 2], HEADS + KVH, 1), 2, 1)
            sin_b = bc(bc(cf[:, C_SIN + HD // 2:C_SIN + HD], HEADS + KVH, 1), 2, 1)
            heads = lambda ap: ap.rearrange("p a (s d) -> p a s d", d=HD)

            def rotate(p):
                dve.wait_ge(s_v, p + 1)
                if p >= 1:
                    dve.wait_ge(s_qlo, p)
                V.tensor_tensor(heads(qcos[:]), heads(qk_ps), cos, ALU.mult).then_inc(s_rope, 1)
                V.tensor_tensor(heads(qsin[:])[:, :, :, 0:8], heads(qk_ps)[:, :, :, 8:16], sin_a, ALU.mult).then_inc(s_rope, 1)
                V.tensor_tensor(heads(qsin[:])[:, :, :, 8:16], heads(qk_ps)[:, :, :, 0:8], sin_b, ALU.mult).then_inc(s_rope, 1)
            def squared_norms(p):
                dve.wait_ge(s_sq, p + 1)
                V.tensor_reduce(ss[:], sq.rearrange("p a (s d) -> p (a s) d", d=HD), AX_X, ALU.add).then_inc(s_nred, 1)

            def guard(p):
                dve.wait_ge(s_nred, p + 1)
                V.tensor_scalar(ss[:], ss[:], 1e-18, None, ALU.max).then_inc(s_norm, 1)

            def heron(p, step):
                dve.wait_ge(s_norm, NORM_STEPS * p + 1 + step)
                if step == 0:
                    dve.wait_ge(s_root, 2 * p + 2)
                    ins = V.reciprocal(inv[:], nrm[:])
                if step == 1:
                    ins = V.tensor_tensor(inv[:], inv[:], ss[:], ALU.mult)
                if step == 2:
                    ins = V.tensor_tensor(inv[:], inv[:], nrm[:], ALU.add)
                if step == 3:
                    ins = V.tensor_scalar(inv[:], inv[:], 0.5, NORM_EPS, ALU.mult, ALU.add)
                if step == 4:
                    ins = V.reciprocal(rn[:], inv[:])
                ins.then_inc(s_norm, 1)

            def stage(p):
                dve.wait_ge(s_norm, NORM_STEPS * (p + 1))
                dve.wait_ge(s_add, p + 1)
                rn_v = bc(rn.rearrange("p (a s) -> p a s", a=2), HD, 3)
                V.tensor_tensor(k_n.rearrange("p (a s) d -> p a s d", a=2), heads(qcos[:])[:, :, HEADS:], rn_v[:, :, HEADS:],
                                ALU.mult).then_inc(s_stage, 1)
                V.tensor_tensor(q_n.rearrange("p (a s) d -> p a s d", a=2), heads(qcos[:])[:, :, 0:HEADS], rn_v[:, :, 0:HEADS],
                                ALU.mult).then_inc(s_stage, 1)
                base = STAGE_STEPS * p
                b = p % 2
                if p >= 2:
                    dve.wait_ge(s_kTp, p - 1)
                k = bc(k_n, 2, 2)
                kv = kst[:, b].rearrange("p a g (l c d) -> p (a g) l c d", l=2, c=2)
                dve.wait_ge(s_stage, base + 1)
                V.tensor_copy(kv[:, :, 0], k).then_inc(s_stage, 1)
                dve.wait_ge(s_stage, base + 3)
                V.tensor_tensor(kv[:, :, 1], k, kv[:, :, 0].bitcast(F32), ALU.subtract).then_inc(s_stage, 1)

            def normalise_outputs(p):
                dve.wait_ge(s_ydT, 2 * (p + 1))
                V.reciprocal(rden.rearrange("p (a s) -> p a s", a=2), y_ps[:, :, :, HD]).then_inc(s_y, 1)
                dve.wait_ge(s_y, 2 * p + 1)
                if p >= 1:
                    dve.wait_ge(s_yTp, p)
                V.tensor_tensor(heads(y[:]), y_ps[:, :, :, 0:HD], bc(rden.rearrange("p (a s) -> p a s", a=2), HD, 3),
                                ALU.mult).then_inc(s_y, 1)

            def residual(p):
                dve.wait_ge(s_proj, 2 * (p + 1))
                x = h[:, 2 * p:2 * p + 2, :]
                V.tensor_tensor(x, x, ps[:, X_BANK, :].rearrange("p (a d) -> p a d", a=2), ALU.add).then_inc(s_res, 1)
                dve.wait_ge(s_res, p + 1)
                statistics(lambda a: h[:, 2 * p + a, :], bn3, mv3, var3, LN_EPS, s_ln3, 5 * p)

            def expert_input(p):
                dve.wait_ge(s_rstd3, p + 1)
                if p >= RBUF:
                    dve.wait_ge(s_scat[p % RBUF], 16 * 2 * TOPK * (p // RBUF))
                for a in range(2):
                    V.tensor_scalar(rows[:, 2 * (p % RBUF) + a, 0:D], h[:, 2 * p + a, :], mv3[:, a, 0:1], rstd3[:, a:a + 1],
                                    ALU.subtract, ALU.mult).then_inc(s_x2, 1)

            def route(p):
                base, r = ROUTE_STEPS * p, 2 * (p % RBUF)
                dve.wait_ge(s_gate, p + 1)
                V.tensor_tensor(sco[:], ps[:, X_BANK, 0:2 * EXPERTS].rearrange("p (a e) -> p a e", a=2),
                                bc(bg[:], 2, 1), ALU.add).then_inc(s_route, 1)
                dve.wait_ge(s_route, base + 1)
                for a in range(2):
                    V.max(top[:, 2 * p + a, :], sco[:, a, :]).then_inc(s_route, 1)
                for a in range(2):
                    dve.wait_ge(s_route, base + 2 + a)
                    V.max_index(topi[:, a, :], top[:, 2 * p + a, :], sco[:, a, :]).then_inc(s_route, 1)
                dve.wait_ge(s_route, base + 5)
                V.tensor_copy(topf[:], topi[:, :, 0:TOPK]).then_inc(s_route, 1)
                V.tensor_copy(rows[:, r:r + 2, D], cf[:, C_TOK + 2 * p:C_TOK + 2 * p + 2]).then_inc(s_route, 1)
                V.tensor_copy(rows[:, r:r + 2, D + 1], topi[:, :, 0]).then_inc(s_route, 1)
                dve.wait_ge(s_route, base + 6)
                ids = bc(bc(cf[:, C_EID:C_EID + EXPERTS], TOPK, 1), 2, 1)
                V.tensor_tensor(pick[:], ids, bc(topf[:], EXPERTS, 3), ALU.is_equal).then_inc(s_route, 1)
                cbase = CHOSEN_STEPS * p
                if p == 0:
                    dve.wait_ge(s_seen0, 1)
                else:
                    dve.wait_ge(s_before, p)
                    V.tensor_tensor(seen[:, 0, :], seen[:, 1, :], chosen[:, 1, :], ALU.add).then_inc(s_seen0, 1)
                    dve.wait_ge(s_seen0, p + 1)
                dve.wait_ge(s_route, base + 9)
                V.tensor_tensor(chosen[:], pick[:, :, 0, :], pick[:, :, 1, :], ALU.add).then_inc(s_chosen, 1)
                dve.wait_ge(s_chosen, cbase + 1)
                V.tensor_tensor(seen[:, 1, :], seen[:, 0, :], chosen[:, 0, :], ALU.add).then_inc(s_chosen, 1)

            def places(p):
                dve.wait_ge(s_before, p + 1)
                V.tensor_tensor(place[:], ps[:, X_BANK, 0:2 * EXPERTS].rearrange("p (a e) -> p a e", a=2),
                                bc(cf[:, C_ECAP:C_ECAP + EXPERTS], 2, 1), ALU.add).then_inc(s_place, 1)
                dve.wait_ge(s_place, p + 1)
                V.tensor_tensor(picked[:], pick[:], bc(place[:], TOPK, 2), ALU.mult).then_inc(s_picked, 1)
                dve.wait_ge(s_picked, 2 * p + 1)
                V.tensor_reduce(destf[:], picked[:], AX_X, ALU.add).then_inc(s_picked, 1)
                dve.wait_ge(s_picked, 2 * p + 2)
                V.tensor_copy(dest[:, 2 * p:2 * p + 2, :], destf[:]).then_inc(s_dest, 1)

            for i in ITERATIONS:
                p = i + 1
                if live(p):
                    dve.wait_ge(s_xThi, p + 1)
                    if p >= 1:
                        dve.wait_ge(s_qkv, 2 * p)
                    lo_part(xT_lo[:], X_BANK, xT_hi[:], s_xTlo)
                if live(i - 2):
                    expert_input(i - 2)
                if live(i + 2):
                    embedding_norms(i + 2, 0)
                if live(p):
                    squared_norms(p)
                    rotate(p)
                    guard(p)
                if live(i + 2):
                    embedding_norms(i + 2, 1)
                if live(i - 1):
                    normalise_outputs(i - 1)
                for step in range(5):
                    if live(p):
                        heron(p, step)
                    if live(i + 2):
                        embedding_norms(i + 2, step + 2)
                if i == -1:
                    for c in range(PIECES):
                        low_weights(w1_f, c, c + 1)
                if live(i - 2):
                    route(i - 2)
                if live(p):
                    stage(p)
                if live(i + 2):
                    embedding_norms(i + 2, 7)
                if live(i - 2):
                    places(i - 2)
                if live(i - 1):
                    dve.wait_ge(s_yThi, i)
                    if i >= 2:
                        dve.wait_ge(s_proj, 2 * (i - 1))
                    lo_part(yT_lo[:], X_BANK, yT_hi[:], s_yTlo)
                    residual(i - 1)
                if i == PAIRS:
                    for c in range(PIECES):
                        low_weights(w2_f, c, PIECES + c + 1)

            steps = [0]

            def table(ins):
                ins.then_inc(s_table, 1)
                steps[0] += 1
                dve.wait_ge(s_table, steps[0])

            slots = cf[:, C_SLOT:C_SLOT + SLOTS]
            dve.wait_ge(s_before_all, 1)
            V.tensor_copy(cnt[:], ps[:, X_BANK, 0:EXPERTS]).then_inc(s_cnt, 1)
            dve.wait_ge(s_cnt, 1)
            V.tensor_tensor(pad_row[:], cnt[:], cf[:, C_ECAP:C_ECAP + EXPERTS], ALU.add).then_inc(s_padrow, 1)
            table(V.tensor_tensor(over[:], bc(cnt[:], SEQS, 2), bc(cf[:, C_THR:C_THR + SEQS], EXPERTS, 1), ALU.is_gt))
            table(V.tensor_reduce(tiles[:], over[:], AX_X, ALU.add))
            tri = cf[:, C_TRI:C_TRI + EXPERTS * EXPERTS].rearrange("p (a b) -> p a b", a=EXPERTS)
            table(V.tensor_tensor(before_e[:], bc(tiles[:], EXPERTS, 1), tri, ALU.mult))
            table(V.tensor_reduce(ends[:], before_e[:], AX_X, ALU.add))
            table(V.tensor_tensor(past[:], bc(slots, EXPERTS, 2), bc(ends[:], SLOTS, 1), ALU.is_ge))
            table(V.tensor_reduce(slot_e[:], past[:], AX_X, ALU.add))
            table(V.tensor_tensor(past_n[:], past[:], bc(tiles[:], SLOTS, 1), ALU.mult))
            table(V.tensor_reduce(slot_0[:], past_n[:], AX_X, ALU.add))
            table(V.tensor_tensor(slot_0[:], slots, slot_0[:], ALU.subtract))
            table(V.tensor_scalar(slot_r[:], slot_e[:], float(CAP), None, ALU.mult))
            table(V.scalar_tensor_tensor(slot_row[:], slot_0[:], float(P), slot_r[:], ALU.mult, ALU.add))
            table(V.tensor_scalar(slot_col[:], slot_e[:], float(EXPERTS - 1), float(D), ALU.min, ALU.mult))
            assert steps[0] == TABLE_STEPS

            def slot_lo(dst, n, hi, done):
                V.tensor_tensor(dst, ps[:, n, 0:D].rearrange("p (k t) -> p k t", k=KC), hi.bitcast(F32),
                                ALU.subtract).then_inc(done, 1)

            def column(s):
                return dve.value_load(slot_col[0:1, bass.ds(s, 1)], min_val=0, max_val=(EXPERTS - 1) * D)

            dve.wait_ge(s_bias, 32)
            for s in range(-2, SLOTS + 1):
                if s + 2 < SLOTS:
                    m = s + 2
                    dve.wait_ge(s_sxhi, m + 1)
                    if m >= 2:
                        dve.wait_ge(s_up, m - 1)
                    slot_lo(xT_lo[:, :, m % 2, :], m % 2, xT_hi[:, :, m % 2, :], s_sxlo)
                if 0 <= s + 1 < SLOTS:
                    m = s + 1
                    n = m % YBUF
                    if m >= YBUF:
                        dve.wait_ge(s_sent[n], 16 * (m // YBUF))
                    V.tensor_tensor(second[:, n:n + 1], slot_x[:, m % XBUF, D + 1:D + 2], slot_e[:, bass.ds(m, 1)],
                                    ALU.not_equal).then_inc(s_isk, 1)
                    dve.wait_ge(s_up, m + 1)
                    if m >= 2:
                        dve.wait_ge(s_hTp, m - 1)
                    V.tensor_tensor(hid[:, m % 2, :], ps[:, 2 + m % 2, 0:D], b1_f[:, bass.ds(column(m), D)],
                                    ALU.add).then_inc(s_hid, 1)
                    dve.wait_ge(s_isk, m + 1)
                    V.scalar_tensor_tensor(to_row[:, n:n + 1], second[:, n:n + 1], float(TOKENS),
                                           slot_x[:, m % XBUF, D:D + 1], ALU.mult, ALU.add).then_inc(s_to, 1)
                if 0 <= s < SLOTS:
                    b = s % 2
                    dve.wait_ge(s_hThi, s + 1)
                    if s >= 2:
                        dve.wait_ge(s_down, s - 1)
                    V.scalar_tensor_tensor(yT_lo[:, :, b, :], ps[:, 4 + b, 0:D].rearrange("p (k t) -> p k t", k=KC), 0.0,
                                           yT_hi[:, :, b, :].bitcast(F32), ALU.max, ALU.subtract).then_inc(s_hTlo, 1)
                if s >= 1:
                    m = s - 1
                    dve.wait_ge(s_down, m + 1)
                    V.tensor_tensor(slot_y[:, m % YBUF, :], ps[:, 6 + m % 2, 0:D], b2_f[:, bass.ds(column(m), D)],
                                    ALU.add).then_inc(s_ys, 1)

            for t in range(0, SEQS, 2):
                for k in range(TOPK):
                    for u in (t, t + 1):
                        if k == 0:
                            dve.wait_ge(s_back[u % CBUF], 16 * (u // CBUF + 1))
                        else:
                            dve.wait_ge(s_mix, 2 * t + 1 + u - t)
                        V.scalar_tensor_tensor(h[:, u, :], coming[:, u % CBUF, k, :], top[:, u, k:k + 1], h[:, u, :],
                                               ALU.mult, ALU.add).then_inc(s_mix, 1)


def constants():
    cf = np.zeros((P, C_WIDTH), np.float32)
    cf[:, C_ID:C_ID + P] = np.eye(P)
    theta = (1.0 / np.float32(10000.0) ** (np.arange(0, HD, 2, dtype=np.float32) / np.float32(HD))).astype(np.float32)
    angle = np.arange(P, dtype=np.float32)[:, None] * theta
    cf[:, C_COS:C_COS + HD] = np.tile(np.cos(angle), 2)
    cf[:, C_SIN:C_SIN + HD] = np.concatenate([-np.sin(angle), np.sin(angle)], 1)
    cf[:, C_ECAP:C_ECAP + EXPERTS] = np.arange(EXPERTS) * CAP
    cf[:, C_EID:C_EID + EXPERTS] = np.arange(EXPERTS)
    cf[:, C_SLOT:C_SLOT + SLOTS] = np.arange(SLOTS)
    cf[:, C_THR:C_THR + SEQS] = np.arange(SEQS) * P
    cf[:, C_TRI:C_TRI + EXPERTS * EXPERTS] = np.tril(np.ones((EXPERTS, EXPERTS))).ravel()
    cf[:, C_TOK:C_TOK + SEQS] = np.arange(SEQS) * P + np.arange(P)[:, None]
    cb = np.zeros((P, B_WIDTH), np.float32)
    cb[:, B_ID:B_ID + P] = np.eye(P)
    cb[:, B_BEFORE:B_BEFORE + P] = np.triu(np.ones((P, P)), 1)
    cb[:, B_ONES:B_ONES + P] = 1.0
    cb[:, B_MASK:] = np.tile(np.where(np.arange(P)[:, None] > np.arange(P), MASKED, 0.0), REP)
    return cf, cb.astype(mybir.dt.np(BF16))


def kernel(**inputs):
    import concourse.bacc as bacc
    from concourse.bass_utils import run_bass_kernel_spmd as run

    a = {k: np.asarray(v) for k, v in inputs.items()}
    wq = a["L0_attn_Wq"].reshape(KVH, REP, HD, D).transpose(1, 0, 2, 3).reshape(D, D)
    w_qkv = np.concatenate([wq, a["L0_attn_Wkv"]], 0).T
    w_proj = a["L0_attn_Wproj"].T.reshape(KVH, REP, HD, D).transpose(1, 0, 2, 3).reshape(D, D)
    cf, cb = constants()
    arrays = {
        "x_idx": a["x"].T, "seg_idx": a["mask_BS_i2_0"].T, "w_word": a["L0_tok_W_word"], "w_pos": a["L0_tok_W_pos"],
        "w_seg": a["L0_tok_W_seg"], "gamma": a["L0_tok_gamma"], "beta": a["L0_tok_beta"], "w_qkv": w_qkv,
        "w_proj": w_proj, "w_gate": a["L0_ffn_W_gate"], "b_gate": a["L0_ffn_b_gate"], "w1": a["L0_ffn_W1"],
        "b1": a["L0_ffn_b1"], "w2": a["L0_ffn_W2"], "b2": a["L0_ffn_b2"], "consts": cf, "consts_bf": cb,
    }
    arrays = {k: np.ascontiguousarray(v) for k, v in arrays.items()}
    nc = bacc.Bacc("TRN2", target_bir_lowering=False, num_devices=1)
    args = [nc.dram_tensor(k, v.shape, mybir.dt.from_np(v.dtype), kind="ExternalInput").ap() for k, v in arrays.items()]
    out = nc.dram_tensor("out", (SEQS, P, D), F32, kind="ExternalOutput").ap()
    attention_moe_program(nc, *args, out)
    result = run(nc, [arrays], core_ids=[0])
    return result.results[0]["out"]
```

```python
from contextlib import ExitStack

import numpy as np

import concourse.bass as bass
from concourse import mybir

ALU = mybir.AluOpType
ACT = mybir.ActivationFunctionType
F32 = mybir.dt.float32
F32R = mybir.dt.float32r
BF16 = mybir.dt.bfloat16
I32 = mybir.dt.int32
U32 = mybir.dt.uint32
AX_X = mybir.AxisListType.X

P = 128
SEQS = 16
PAIRS = SEQS // 2
D = 256
KC = D // P
HEADS, KVH, HD = 16, 4, 16
REP = HEADS // KVH
QK = (HEADS + KVH) * HD
QKV = QK + KVH * HD
EXPERTS, TOPK = 8, 2
TOKENS = SEQS * P
CAP = TOKENS + P
SLOTS = TOKENS * TOPK // P + EXPERTS - 1
SPARE = EXPERTS - 1
ROW = D + 2
NO_TOKEN = float(1 << 20)
LN_EPS, NORM_EPS, TOK_EPS = 1e-5, 1e-6, 1e-6
MASKED = -30000.0
PADV = 160

LN_STEPS, NORM_STEPS, ROPE_STEPS, STAGE_STEPS = 14, 6, 3, 4
ROUTE_STEPS, CHOSEN_STEPS, TABLE_STEPS = 9, 2, 12
XBUF, YBUF, TBUF, CBUF, RBUF = 4, 4, 8, 8, 2

C_ID, C_COS, C_SIN = 0, 128, 144
C_ECAP, C_EID = 160, 168
C_SLOT = 176
C_THR = C_SLOT + SLOTS
C_TRI = C_THR + SEQS
C_TOK = C_TRI + EXPERTS * EXPERTS
C_HALF = C_TOK + SEQS
C_WIDTH = C_HALF + 2
B_ID, B_BEFORE, B_ONES, B_MASK = 0, 128, 256, 384
B_WIDTH = 384 + REP * P


LOADED = 13


class SlotValues:
    def __init__(self, nc, table, engine, max_val):
        self.nc, self.table, self.engine, self.max_val, self.values = nc, table, engine, max_val, {}

    def __call__(self, s):
        if s not in self.values:
            a, b = s, min(s + (LOADED if s else XBUF), SLOTS)
            _, values = self.nc.values_load_multi_w_load_instructions(
                self.table[0:1, a:b], engines=[self.engine], min_val=0, max_val=self.max_val,
                skip_runtime_bounds_check_because="the table is worked out within the bounds")
            self.values = dict(zip(range(a, b), values)) | {k: v for k, v in self.values.items() if k > a - 3}
        return self.values[s]


def attention_moe_program(nc, x_idx, seg_idx, w_word, w_pos, w_seg, gamma, beta, w_qkv, w_proj,
                          w_gate, b_gate, w1, b1, w2, b2, consts, consts_bf, out):
    x_rows = nc.dram_tensor("x_rows", (EXPERTS * CAP + SPARE * P, ROW), F32).ap()
    y_rows = nc.dram_tensor("y_rows", (TOPK * TOKENS, D), F32).ap()

    with ExitStack() as ctx:
        def sb(name, shape, dt=F32):
            return ctx.enter_context(nc.sbuf_tensor(name, shape, dt))

        def sem(name):
            return ctx.enter_context(nc.semaphore(name))

        cf = sb("cf", [P, C_WIDTH])
        cb = sb("cb", [P, B_WIDTH], BF16)
        ident = cf[:, C_ID:C_ID + P]
        gam = sb("gam", [P, D])
        bet = sb("bet", [P, D])
        bg = sb("bg", [P, EXPERTS])
        widx = sb("widx", [P, SEQS], I32)
        sidx = sb("sidx", [P, SEQS], I32)
        h = sb("h", [P, SEQS, D])
        rows = sb("rows", [P, 2 * RBUF, ROW])
        raw = sb("raw", [P, KC, EXPERTS, D])
        wq_hi = sb("wq_hi", [P, KC, QKV], F32R)
        wq_lo = sb("wq_lo", [P, KC, QKV], F32R)
        wp_hi = sb("wp_hi", [P, KC, D], F32R)
        wp_lo = sb("wp_lo", [P, KC, D], F32R)
        wg = sb("wg", [P, KC, EXPERTS])
        w1_hi = sb("w1_hi", [P, KC, EXPERTS * D], F32R)
        w1_lo = sb("w1_lo", [P, KC, EXPERTS * D], F32R)
        w2_hi = sb("w2_hi", [P, KC, EXPERTS * D], F32R)
        w2_lo = sb("w2_lo", [P, KC, EXPERTS * D], F32R)
        half = sb("half", [P, 2])

        bn = sb("bn", [P, 2, 6])
        mv = sb("mv", [P, 2, 2])
        rstd = sb("rstd", [P, 2])
        var_e = sb("var_e", [P, 2])
        xn = sb("xn", [P, 2, 2, D])
        xT_hi = sb("xT_hi", [P, KC, 2, P], F32R)
        xT_lo = sb("xT_lo", [P, KC, 2, P], F32R)
        sq = sb("sq", [P, 2, QK])
        ss = sb("ss", [P, 2 * (HEADS + KVH)])
        lnss = sb("lnss", [P, 2 * (HEADS + KVH)])
        nrm = sb("nrm", [P, 2 * (HEADS + KVH)])
        inv = sb("inv", [P, 2 * (HEADS + KVH)])
        rn = sb("rn", [P, 2 * (HEADS + KVH)])
        qcos = sb("qcos", [P, 2, QK])
        qsin = sb("qsin", [P, 2, QK])
        qst = sb("qst", [P, 2, 2, HEADS, 4 * HD], F32R)
        kst = sb("kst", [P, 2, 2, KVH, 4 * HD], F32R)
        vz = sb("vz", [P, 2, 2, KVH * PADV])
        kpad = sb("kpad", [P, 2, KVH, P], F32R)
        qT = sb("qT", [P, 2, 2, REP * P], F32R)
        prob = sb("prob", [P, 2, KVH, REP * P])
        yd = sb("yd", [P, 2, REP * P])
        rden = sb("rden", [P, 2 * HEADS])
        y = sb("y", [P, 2, D])
        yT_hi = sb("yT_hi", [P, KC, 2, P], F32R)
        yT_lo = sb("yT_lo", [P, KC, 2, P], F32R)
        x2T = sb("x2T", [P, KC, 2, P])
        sco = sb("sco", [P, 2, EXPERTS])
        top = sb("top", [P, SEQS, 8])
        topi = sb("topi", [P, 2, 8], U32)
        topf = sb("topf", [P, 2, TOPK])
        pick = sb("pick", [P, 2, TOPK, EXPERTS])
        chosen = sb("chosen", [P, 2, EXPERTS], BF16)
        seen = sb("seen", [P, 2, EXPERTS], BF16)
        place = sb("place", [P, 2, EXPERTS])
        picked = sb("picked", [P, 2, TOPK, EXPERTS])
        destf = sb("destf", [P, 2, TOPK])
        dest = sb("dest", [P, SEQS, TOPK], I32)
        pad_rows = sb("pad_rows", [P, ROW])
        bn3 = sb("bn3", [P, 2, 6])
        mv3 = sb("mv3", [P, 2, 2])
        rstd3 = sb("rstd3", [P, 2])
        var3 = sb("var3", [P, 2])
        cnt = sb("cnt", [P, EXPERTS])
        over = sb("over", [P, EXPERTS, SEQS])
        tiles = sb("tiles", [P, EXPERTS])
        before_e = sb("before_e", [P, EXPERTS, EXPERTS])
        ends = sb("ends", [P, EXPERTS])
        slot_e = sb("slot_e", [P, SLOTS])
        slot_0 = sb("slot_0", [P, SLOTS])
        slot_r = sb("slot_r", [P, SLOTS])
        slot_row = sb("slot_row", [P, SLOTS], I32)
        slot_col = sb("slot_col", [P, SLOTS], I32)
        pad_row = sb("pad_row", [P, EXPERTS], I32)
        second = sb("second", [P, TBUF])
        to_row = sb("to_row", [P, TBUF], I32)

        ps = ctx.enter_context(nc.psum_tensor("ps", [P, 8, 512], F32))

        s_const = sem("s_const")
        s_widx, s_sidx = sem("s_widx"), sem("s_sidx")
        s_pos = [sem(f"s_pos{n}") for n in range(5)]
        s_word = [sem(f"s_word{t}") for t in range(SEQS)]
        s_emb = [sem(f"s_emb{t}") for t in range(SEQS)]
        s_wraw = sem("s_wraw")
        s_w1raw, s_w2raw = sem("s_w1raw"), sem("s_w2raw")
        s_hi, s_split_hi, s_split = sem("s_hi"), sem("s_split_hi"), sem("s_split")
        s_filled, s_half, s_seen0, s_nred, s_root = sem("s_filled"), sem("s_half"), sem("s_seen0"), sem("s_nred"), sem("s_root")
        s_qhi = sem("s_qhi")
        s_place, s_picked, s_rstd3 = sem("s_place"), sem("s_picked"), sem("s_rstd3")
        s_init = sem("s_init")
        s_ln = sem("s_ln")
        s_rstd = sem("s_rstd")
        s_xn = sem("s_xn")
        s_xTp, s_xThi, s_xTlo = sem("s_xTp"), sem("s_xThi"), sem("s_xTlo")
        s_qkv = sem("s_qkv")
        s_sq, s_rope, s_norm, s_v = sem("s_sq"), sem("s_rope"), sem("s_norm"), sem("s_v")
        s_stage = sem("s_stage")
        s_kTp, s_kT = sem("s_kTp"), sem("s_kT")
        s_qTp, s_qT = sem("s_qTp"), sem("s_qT")
        s_score, s_prob = sem("s_score"), sem("s_prob")
        s_pv, s_yd = sem("s_pv"), sem("s_yd")
        s_ydT, s_y = sem("s_ydT"), sem("s_y")
        s_yTp, s_yThi, s_yTlo = sem("s_yTp"), sem("s_yThi"), sem("s_yTlo")
        s_proj, s_res = sem("s_proj"), sem("s_res")
        s_ln3, s_x2 = sem("s_ln3"), sem("s_x2")
        s_x2Tp, s_x2T = sem("s_x2Tp"), sem("s_x2T")
        s_gate, s_route, s_chosen, s_before, s_dest = (sem("s_gate"), sem("s_route"), sem("s_chosen"),
                                                       sem("s_before"), sem("s_dest"))
        s_scat = [sem(f"s_scat{n}") for n in range(RBUF)]
        s_before_all, s_table = sem("s_before_all"), sem("s_table")
        s_pads = sem("s_pads")
        s_bias, s_padrow, s_add = sem("s_bias"), sem("s_padrow"), sem("s_add")
        s_qlo, s_cnt, s_blank = sem("s_qlo"), sem("s_cnt"), sem("s_blank")
        s_slot = [sem(f"s_slot{n}") for n in range(XBUF)]
        s_sxp, s_sxhi, s_sxlo = sem("s_sxp"), sem("s_sxhi"), sem("s_sxlo")
        s_up, s_hid = sem("s_up"), sem("s_hid")
        s_hTp, s_hThi, s_hTlo = sem("s_hTp"), sem("s_hThi"), sem("s_hTlo")
        s_down, s_ys = sem("s_down"), sem("s_ys")
        s_isk, s_to = sem("s_isk"), sem("s_to")
        s_sent = [sem(f"s_sent{n}") for n in range(YBUF)]
        s_back = [sem(f"s_back{n}") for n in range(CBUF)]
        s_mix, s_out = sem("s_mix"), sem("s_out")

        def bc(ap, n, axis):
            ap = ap.unsqueeze(axis)
            shape = list(ap.shape)
            shape[axis] = n
            return ap.broadcast_to(shape)

        def part(t, *shape):
            flat = t.rearrange("p a c -> p (a c)") if len(t.shape) == 3 else t.rearrange("p b a c -> p (b a c)")
            return flat[:, 0:shape[0] * shape[1]].rearrange("p (m n) -> p m n", m=shape[0])

        past, past_n = part(qcos, SLOTS, EXPERTS), part(qsin, SLOTS, EXPERTS)
        slot_x, slot_y, hid = part(vz, XBUF, ROW), part(yd, YBUF, D), y
        prob_f = prob.rearrange("p a g n -> p (a g n)")
        b1_f, b2_f = prob_f[:, 0:EXPERTS * D], prob_f[:, EXPERTS * D:2 * EXPERTS * D]
        coming = raw.rearrange("p k e d -> p (k e d)").rearrange("p (c k d) -> p c k d", c=CBUF, k=TOPK)
        POS = [(0, 2), (2, 4), (4, 8), (8, 12), (12, SEQS)]
        def bank(n, cols=512):
            return ps[:, n, 0:cols]

        S_BANK, Q_BANK, X_BANK, V_BANK, QKV_BANK = 0, 2, 4, 5, 6
        qk_ps = ps[:, QKV_BANK:QKV_BANK + 2, 0:QK]
        v_ps = ps[:, QKV_BANK:QKV_BANK + 2, QK:QKV].rearrange("p a (g d) -> p a g d", d=HD)
        y_ps = ps[:, Q_BANK:Q_BANK + 2, :].rearrange("p a (s c) -> p a s c", c=2 * HD)
        vz_v = vz.rearrange("p b a (g c) -> p b a g c", c=PADV)
        qk_n = qsin.rearrange("p a n -> p (a n)")
        q_n = qk_n[:, 0:2 * HEADS * HD].rearrange("p (s d) -> p s d", d=HD)
        k_n = qk_n[:, 2 * HEADS * HD:].rearrange("p (s d) -> p s d", d=HD)

        def q_stage(b):
            v = qst[:, b].rearrange("p a s (c l d) -> p (a s) c l d", c=2, l=2)
            return v[:, :, :, 0], v[:, :, 0, 1], v[:, :, 1, 1]

        raw_f = raw.rearrange("p k e d -> p (k e d)")
        w1_f = [w1_hi.rearrange("p k n -> p (k n)"), w1_lo.rearrange("p k n -> p (k n)")]
        w2_f = [w2_hi.rearrange("p k n -> p (k n)"), w2_lo.rearrange("p k n -> p (k n)")]
        PIECES = PAIRS // 2
        PIECE = KC * EXPERTS * D // PIECES
        ITERATIONS = range(-2, PAIRS + 2)

        def live(p):
            return 0 <= p < PAIRS

        def write_padding(eng, first, end):
            eng.wait_ge(s_padrow, 1)
            _, ends = nc.values_load_multi_w_load_instructions(
                pad_row[0:1, first:end], engines=[eng.engine], min_val=0, max_val=EXPERTS * CAP - P,
                skip_runtime_bounds_check_because="an expert has between none and all of the tokens")
            for at in ends:
                eng.dma_start(x_rows[bass.ds(at, P), :], pad_rows[:]).then_inc(s_pads, 16)

        block = ctx.enter_context(nc.Block())

        @block.sync
        def _(sp):
            sp.dma_start(widx[:], x_idx).then_inc(s_widx, 16)

            def positions(n):
                a, b = POS[n]
                sp.dma_start(h[:, a:b, :], bc(w_pos, b - a, 1)).then_inc(s_pos[n], 16)

            positions(0)
            sp.dma_start(sidx[:], seg_idx).then_inc(s_sidx, 16)
            sp.dma_start(raw_f[:, 0:KC * QKV].rearrange("p (k n) -> p k n", k=KC),
                         w_qkv.rearrange("(k p) n -> p k n", p=P)).then_inc(s_wraw, 16)
            positions(1)
            sp.dma_start(gam[:], gamma.partition_broadcast(P)).then_inc(s_const, 16)
            sp.dma_start(bet[:], beta.partition_broadcast(P)).then_inc(s_const, 16)
            sp.wait_ge(s_emb[1], 16)
            positions(2)
            sp.wait_ge(s_emb[3], 16)
            for n in range(3, len(POS)):
                positions(n)
            sp.wait_ge(s_emb[5], 16)
            sp.wait_ge(s_hi, 4)
            for k in range(KC):
                sp.dma_start(raw[:, k], w1.rearrange("e (k p) d -> k p e d", p=P)[k]).then_inc(s_w1raw, 16)
            sp.wait_ge(s_split, 8)
            for k in range(KC):
                sp.dma_start(raw[:, k], w2.rearrange("e (k p) d -> k p e d", p=P)[k]).then_inc(s_w2raw, 16)
            sp.wait_ge(s_pv, 2 * PAIRS)
            sp.dma_start(b1_f, b1.rearrange("e d -> (e d)").partition_broadcast(P)).then_inc(s_bias, 16)
            sp.dma_start(b2_f, b2.rearrange("e d -> (e d)").partition_broadcast(P)).then_inc(s_bias, 16)
            write_padding(sp, 0, 4)
            sp.wait_ge(s_table, TABLE_STEPS)

            def slot_at(s):
                return sp.value_load(slot_row[0:1, bass.ds(s, 1)], min_val=0, max_val=EXPERTS * CAP + (SPARE - 1) * P)

            def load_slot(row, n):
                sp.dma_start(slot_x[:, n, :], x_rows[bass.ds(row, P), :]).then_inc(s_slot[n], 16)

            def next_slot(s, n):
                row = slot_at(s)
                sp.wait_ge(s_sxp, s - XBUF + 1)
                sp.wait_ge(s_to, s - XBUF + 1)
                load_slot(row, n)

            first_rows = [slot_at(s) for s in range(XBUF)]
            sp.wait_ge(s_pads, 16 * (EXPERTS + 1))
            for n in range(RBUF):
                sp.wait_ge(s_scat[n], 16 * 2 * TOPK * (PAIRS // RBUF))
            for s in range(XBUF):
                load_slot(first_rows[s], s)
            whole = SLOTS - SLOTS % XBUF
            with sp.Fori(XBUF, whole, XBUF) as s:
                for n in range(XBUF):
                    next_slot(s + n, n)
            for s in range(whole, SLOTS):
                next_slot(s, s % XBUF)

            for n in range(YBUF):
                sp.wait_ge(s_sent[n], 16 * len(range(n, SLOTS, YBUF)))
            back = y_rows.rearrange("(k t p) d -> t p k d", k=TOPK, p=P)
            for t in range(SEQS):
                n = t % CBUF
                if t >= CBUF:
                    sp.wait_ge(s_mix, 2 * (t - CBUF + 2 - t % 2))
                sp.dma_start(coming[:, n], back[t]).then_inc(s_back[n], 16)

        @block.gpsimd
        def _(pool):
            def gather(t, table, idx, done):
                nc.gpsimd.indirect_dma_start(
                    out=h[:, t, :], out_offset=None, in_=table,
                    in_offset=bass.IndirectOffsetOnAxis(ap=idx[:, t:t + 1], axis=0),
                    compute_op=ALU.add).then_inc(done, 16)

            def words(t):
                pool.wait_ge(s_pos[max(n for n, (a, b) in enumerate(POS) if a <= t)], 16)
                gather(t, w_word, widx, s_word[t])

            def segments(t):
                pool.wait_ge(s_word[t], 16)
                gather(t, w_seg, sidx, s_emb[t])

            pool.wait_ge(s_widx, 16)
            for t in range(2):
                words(t)
            nc.gpsimd.memset(half[:], -0.5).then_inc(s_half, 1)
            pool.wait_ge(s_sidx, 16)
            for t in range(2):
                segments(t)
            for t in range(2, 4):
                words(t)
            pool.wait_ge(s_half, 1)

            def power(out_ap, in_ap, done):
                nc.gpsimd.tensor_tensor(out_ap, in_ap, half[:, 0:2], ALU.pow).then_inc(done, 1)

            def embedding_power(p, steps):
                pool.wait_ge(s_ln, LN_STEPS * p + steps)
                power(rstd[:], var_e[:], s_rstd)

            embedding_power(0, 5)
            for t in range(2, 4):
                segments(t)
            embedding_power(0, 14)
            nc.gpsimd.memset(kpad[:].bitcast(F32), 0.0).then_inc(s_init, 1)
            embedding_power(1, 5)
            nc.gpsimd.memset(vz[:], 0.0).then_inc(s_filled, 1)
            nc.gpsimd.memset(pad_rows[:, 0:D], 0.0).then_inc(s_filled, 1)
            nc.gpsimd.memset(pad_rows[:, D:D + 1], NO_TOKEN).then_inc(s_filled, 1)
            nc.gpsimd.memset(pad_rows[:, D + 1:ROW], 0.0).then_inc(s_filled, 1)
            embedding_power(1, 14)
            pool.wait_ge(s_filled, 4)
            nc.gpsimd.memset(vz_v[:, :, :, :, HD:HD + 1], 1.0).then_inc(s_init, 1)
            for t in range(4, 6):
                words(t)

            for i in range(-1, PAIRS + 2):
                later = [t for t in (2 * (i + 3), 2 * (i + 3) + 1) if t < SEQS]
                if live(i - 2) and i <= PAIRS:
                    pool.wait_ge(s_ln3, 5 * (i - 1))
                    power(rstd3[:], var3[:], s_rstd3)
                if live(i + 2) and i >= 0:
                    embedding_power(i + 2, 5)
                if i >= 0:
                    for t in later:
                        words(t)
                if live(i + 1):
                    pool.wait_ge(s_rope, ROPE_STEPS * (i + 2))
                    nc.gpsimd.tensor_tensor(qcos[:], qcos[:], qsin[:], ALU.add).then_inc(s_add, 1)
                if live(i + 2) and i >= 0:
                    embedding_power(i + 2, 14)
                if live(i + 1):
                    p = i + 1
                    q_hi, q_lo, _ = q_stage(p % 2)
                    pool.wait_ge(s_qhi, p + 1)
                    nc.gpsimd.tensor_tensor(q_lo, q_n, q_hi[:, :, 0].bitcast(F32), ALU.subtract).then_inc(s_qlo, 1)
                for t in later:
                    segments(t)
                if live(i - 2):
                    if i == PAIRS:
                        pool.wait_ge(s_ln3, 5 * PAIRS)
                        power(rstd3[:], var3[:], s_rstd3)
                    p = i - 2
                    pool.wait_ge(s_dest, p + 1)
                    for t in (2 * p, 2 * p + 1):
                        for k in range(TOPK):
                            nc.gpsimd.indirect_dma_start(
                                out=x_rows, out_offset=bass.IndirectOffsetOnAxis(ap=dest[:, t, k:k + 1], axis=0),
                                in_=rows[:, t % (2 * RBUF), :], in_offset=None).then_inc(s_scat[p % RBUF], 16)

            def send(n, t):
                nc.gpsimd.indirect_dma_start(
                    out=y_rows, out_offset=bass.IndirectOffsetOnAxis(ap=to_row[:, t:t + 1], axis=0),
                    in_=slot_y[:, n, :], in_offset=None, bounds_check=TOPK * TOKENS - 1,
                    oob_is_err=False).then_inc(s_sent[n], 16)

            for s in range(SLOTS):
                pool.wait_ge(s_ys, s + 1)
                pool.wait_ge(s_to, s + 1)
                send(s % YBUF, s % TBUF)

        @block.tensor
        def _(pe):
            def split_product(out_ap, lhs, rhs, start=True, stop=True):
                n = len(lhs)
                for k in range(n):
                    (ah, al), (bh, bl) = lhs[k], rhs[k]
                    nc.tensor.matmul(out_ap, ah, bh, start=start and k == 0, stop=False)
                    nc.tensor.matmul(out_ap, ah, bl, start=False, stop=False)
                    last = nc.tensor.matmul(out_ap, al, bh, start=False, stop=stop and k == n - 1)
                return last

            def transpose_pair(n, src, done):
                for k in range(KC):
                    for a in range(2):
                        c = (2 * k + a) * P
                        last = nc.tensor.transpose(ps[:, n, c:c + P], src(a)[:, k * P:(k + 1) * P], ident)
                last.then_inc(done, 1)

            def q_transposes(p, a):
                for pr in range(2):
                    m = 4 * p + 2 * a + pr
                    if pr == 0:
                        pe.wait_ge(s_qlo, p + 1)
                        pe.wait_ge(s_blank, 2)
                    if m >= 2:
                        pe.wait_ge(s_qT, m - 1)
                    for j in range(REP):
                        two = qst[:, p % 2, a, 4 * j + 2 * pr:4 * j + 2 * pr + 2, :].rearrange("p s c -> p (s c)")
                        last = nc.tensor.transpose(ps[:, Q_BANK + pr, j * P:(j + 1) * P], two.bitcast(F32), ident)
                    last.then_inc(s_qTp, 1)

            def k_transposes(p):
                pe.wait_ge(s_stage, STAGE_STEPS * (p + 1))
                if p >= 1:
                    pe.wait_ge(s_yd, 2 * p)
                for a in range(2):
                    for pr in range(2):
                        c = (2 * a + pr) * P
                        keys = kst[:, p % 2, a, 2 * pr:2 * pr + 2, :].rearrange("p g c -> p (g c)").bitcast(F32)
                        last = nc.tensor.transpose(ps[:, V_BANK, c:c + P], keys, ident)
                last.then_inc(s_kTp, 1)

            def scores(p, a, groups):
                for g in groups:
                    m = 8 * p + 4 * a + g
                    if g == 0:
                        pe.wait_ge(s_kT, 2 * (p + 1))
                        pe.wait_ge(s_const, 16 * 6)
                    pe.wait_ge(s_qT, 4 * p + 2 * a + g // 2 + 1)
                    if m >= 2:
                        pe.wait_ge(s_prob, m - 1)
                    o = bank(S_BANK + g % 2)
                    nc.tensor.matmul(o, kpad[:, a, g, :], qT[:, a, g // 2, :], start=True, stop=False)
                    nc.tensor.matmul(o, cb[:, B_ID:B_ID + P], cb[:, B_MASK:B_MASK + REP * P],
                                     start=False, stop=True).then_inc(s_score, 1)

            def values(p, a, groups):
                if groups[0] == 0 and a == 0:
                    pe.wait_ge(s_kT, 2 * (p + 1))
                    pe.wait_ge(s_v, p + 1)
                    pe.wait_ge(s_init, 2)
                if groups[0] == 0 and a == 1:
                    pe.wait_ge(s_yd, 2 * p + 1)
                for g in groups:
                    pe.wait_ge(s_prob, 8 * p + 4 * a + g + 1)
                    ins = nc.tensor.matmul(bank(V_BANK), vz[:, p % 2, a, g * P:(g + 1) * P], prob[:, a, g, :],
                                           start=(g == 0), stop=(g == KVH - 1))
                    if g == KVH - 1:
                        ins.then_inc(s_pv, 1)

            def gate(p, n):
                pe.wait_ge(s_x2T, p + 1)
                for a in range(2):
                    for k in range(KC):
                        last = nc.tensor.matmul(ps[:, n, EXPERTS * a:EXPERTS * (a + 1)], x2T[:, k, a, :],
                                                wg[:, k, :], start=(k == 0), stop=(k == KC - 1))
                last.then_inc(s_gate, 1)

            def before(p, n):
                pe.wait_ge(s_chosen, CHOSEN_STEPS * (p + 1))
                o = ps[:, n, 0:2 * EXPERTS]
                nc.tensor.matmul(o, cb[:, B_BEFORE:B_BEFORE + P], chosen.rearrange("p a e -> p (a e)"),
                                 start=True, stop=False)
                nc.tensor.matmul(o, cb[:, B_ONES:B_ONES + P], seen.rearrange("p a e -> p (a e)"),
                                 start=False, stop=True).then_inc(s_before, 1)

            def output_transposes(p):
                for a in range(2):
                    pe.wait_ge(s_yd, 2 * p + a + 1)
                    if a == 0:
                        pe.wait_ge(s_qT, 4 * p + 6 if live(p + 1) else 4 * p + 4)
                    for j in range(REP):
                        last = nc.tensor.transpose(ps[:, Q_BANK + a, j * P:(j + 1) * P],
                                                   yd[:, a, j * P:(j + 1) * P], ident)
                    last.then_inc(s_ydT, 1)

            pe.wait_ge(s_const, 16 * 6)
            def expert_transposes(p, n):
                pe.wait_ge(s_x2, 2 * (p + 1))
                transpose_pair(n, lambda a: rows[:, 2 * (p % RBUF) + a, 0:D], s_x2Tp)

            def normalised_transposes(p):
                pe.wait_ge(s_y, 2 * (p + 1))
                if 1 <= p < PAIRS - 1:
                    pe.wait_ge(s_place, p)
                transpose_pair(X_BANK, lambda a: y[:, a, :], s_yTp)

            def projection(p):
                pe.wait_ge(s_yTlo, p + 1)
                pe.wait_ge(s_yThi, p + 1)
                if p == PAIRS - 1:
                    pe.wait_ge(s_res, p)
                for a in range(2):
                    last = split_product(ps[:, QKV_BANK, a * D:(a + 1) * D],
                                         [(yT_hi[:, k, a, :], yT_lo[:, k, a, :]) for k in range(KC)],
                                         [(wp_hi[:, k, :], wp_lo[:, k, :]) for k in range(KC)])
                    last.then_inc(s_proj, 1)

            def attention_transposes(p):
                pe.wait_ge(s_xn, 2 * (p + 1))
                if p == 1:
                    pe.wait_ge(s_xThi, 1)
                    pe.wait_ge(s_xTlo, 1)
                transpose_pair(X_BANK, lambda a: xn[:, p % 2, a, :], s_xTp)

            def queries_keys_values(p):
                pe.wait_ge(s_xTlo, p + 1)
                pe.wait_ge(s_xThi, p + 1)
                if p == 0:
                    pe.wait_ge(s_hi, 4)
                else:
                    pe.wait_ge(s_v, p)
                    pe.wait_ge(s_rope, ROPE_STEPS * p)
                if p >= 3:
                    pe.wait_ge(s_res, p - 2)
                for a in range(2):
                    last = split_product(ps[:, QKV_BANK + a, 0:QKV],
                                         [(xT_hi[:, k, a, :], xT_lo[:, k, a, :]) for k in range(KC)],
                                         [(wq_hi[:, k, :], wq_lo[:, k, :]) for k in range(KC)])
                    last.then_inc(s_qkv, 1)

            for p in range(2):
                attention_transposes(p)
                queries_keys_values(p)
            for i in range(PAIRS):
                q_transposes(i, 0)
                k_transposes(i)
                if live(i - 2):
                    projection(i - 2)
                scores(i, 0, range(0, 1))
                if live(i + 1) and i >= 1:
                    attention_transposes(i + 1)
                scores(i, 0, range(1, 2))
                if live(i - 1):
                    output_transposes(i - 1)
                if live(i + 1) and i >= 1:
                    queries_keys_values(i + 1)
                if live(i):
                    scores(i, 0, range(2, KVH))
                if live(i - 2):
                    expert_transposes(i - 2, X_BANK)
                if live(i):
                    values(i, 0, range(0, 2))
                    if i >= 1:
                        pe.wait_ge(s_y, 2 * i)
                    q_transposes(i, 1)
                    values(i, 0, range(2, KVH))
                if live(i):
                    scores(i, 1, range(0, 2))
                if live(i - 2):
                    gate(i - 2, X_BANK)
                if live(i):
                    scores(i, 1, range(2, KVH))
                    values(i, 1, range(0, 3))
                if live(i - 2):
                    before(i - 2, X_BANK)
                if live(i):
                    values(i, 1, range(3, KVH))
                if live(i - 1):
                    normalised_transposes(i - 1)

            output_transposes(PAIRS - 1)
            projection(PAIRS - 2)
            normalised_transposes(PAIRS - 1)
            projection(PAIRS - 1)
            expert_transposes(PAIRS - 2, S_BANK)
            gate(PAIRS - 2, S_BANK)
            expert_transposes(PAIRS - 1, S_BANK + 1)
            before(PAIRS - 2, S_BANK)
            gate(PAIRS - 1, S_BANK + 1)
            before(PAIRS - 1, S_BANK + 1)

            nc.tensor.matmul(ps[:, X_BANK, 0:EXPERTS], cb[:, B_ONES:B_ONES + P], seen[:, 1, :],
                             start=True, stop=False)
            nc.tensor.matmul(ps[:, X_BANK, 0:EXPERTS], cb[:, B_ONES:B_ONES + P], chosen[:, 1, :],
                             start=False, stop=True).then_inc(s_before_all, 1)

            SX, SH, ST, SY = 0, 2, 4, 6

            def slot_transposes(s, b, n):
                pe.wait_ge(s_slot[n], (s // XBUF + 1) * 16)
                if s >= 2:
                    pe.wait_ge(s_sxhi, s - 1)
                    pe.wait_ge(s_sxlo, s - 1)
                for k in range(KC):
                    last = nc.tensor.transpose(ps[:, SX + b, k * P:(k + 1) * P], slot_x[:, n, k * P:(k + 1) * P], ident)
                last.then_inc(s_sxp, 1)

            def up(s, b, col):
                pe.wait_ge(s_sxhi, s + 1)
                pe.wait_ge(s_sxlo, s + 1)
                if s >= 2:
                    pe.wait_ge(s_hid, s - 1)
                split_product(ps[:, SH + b, 0:D], [(xT_hi[:, k, b, :], xT_lo[:, k, b, :]) for k in range(KC)],
                              [(w1_hi[:, k, bass.ds(col, D)], w1_lo[:, k, bass.ds(col, D)]) for k in range(KC)]
                              ).then_inc(s_up, 1)

            def hidden_transposes(s, b):
                pe.wait_ge(s_hid, s + 1)
                if s >= 2:
                    pe.wait_ge(s_hThi, s - 1)
                    pe.wait_ge(s_hTlo, s - 1)
                for k in range(KC):
                    last = nc.tensor.transpose(ps[:, ST + b, k * P:(k + 1) * P], hid[:, b, k * P:(k + 1) * P], ident)
                last.then_inc(s_hTp, 1)

            def down(s, b, col):
                pe.wait_ge(s_hThi, s + 1)
                pe.wait_ge(s_hTlo, s + 1)
                if s == 0:
                    pe.wait_ge(s_split, 16)
                if s >= 2:
                    pe.wait_ge(s_ys, s - 1)
                split_product(ps[:, SY + b, 0:D], [(yT_hi[:, k, b, :], yT_lo[:, k, b, :]) for k in range(KC)],
                              [(w2_hi[:, k, bass.ds(col, D)], w2_lo[:, k, bass.ds(col, D)]) for k in range(KC)]
                              ).then_inc(s_down, 1)

            pe.wait_ge(s_table, TABLE_STEPS)
            pe.wait_ge(s_split, 8)
            column = SlotValues(nc, slot_col, mybir.EngineType.PE, (EXPERTS - 1) * D)
            for s in range(-2, SLOTS + 1):
                if s + 2 < SLOTS:
                    slot_transposes(s + 2, s % 2, (s + 2) % XBUF)
                if 0 <= s + 1 < SLOTS:
                    up(s + 1, (s + 1) % 2, column(s + 1))
                if 0 <= s < SLOTS:
                    hidden_transposes(s, s % 2)
                if s >= 1:
                    down(s - 1, (s - 1) % 2, column(s - 1))

        @block.scalar
        def _(act):
            act.preload_act_table_set("natural_log_exp_and_others")
            act.dma_start(cf[:], consts).then_inc(s_const, 16)
            act.dma_start(cb[:], consts_bf).then_inc(s_const, 16)
            act.dma_start(raw_f[:, KC * QKV:KC * (QKV + D)].rearrange("p (k n) -> p k n", k=KC),
                          w_proj.rearrange("(k p) n -> p k n", p=P)).then_inc(s_wraw, 16)
            act.dma_start(bg[:], b_gate.partition_broadcast(P)).then_inc(s_const, 16)
            act.dma_start(wg[:], w_gate.rearrange("(k p) e -> p k e", p=P)).then_inc(s_const, 16)

            def copy(out_ap, in_ap, done):
                nc.scalar.activation(out_ap, in_ap, ACT.Copy).then_inc(done, 1)

            def x_bank(n=X_BANK):
                return ps[:, n, :].rearrange("p (k a t) -> p k a t", k=KC, a=2)

            def q_copies(p, a):
                for pr in range(2):
                    m = 4 * p + 2 * a + pr
                    act.wait_ge(s_qTp, m + 1)
                    if p >= 1:
                        act.wait_ge(s_score, 8 * (p - 1) + 4 * a + 2 * pr + 2)
                    copy(qT[:, a, pr, :], bank(Q_BANK + pr), s_qT)

            def probabilities(p, a, groups):
                for g in groups:
                    m = 8 * p + 4 * a + g
                    act.wait_ge(s_score, m + 1)
                    if p >= 1 and g == 0:
                        act.wait_ge(s_pv, 2 * (p - 1) + a + 1)
                    nc.scalar.activation(prob[:, a, g, :], bank(S_BANK + g % 2), ACT.Exp,
                                         scale=float(HD) ** -0.5).then_inc(s_prob, 1)

            def outputs(p, a):
                act.wait_ge(s_pv, 2 * p + a + 1)
                if p >= 1:
                    act.wait_ge(s_ydT, 2 * (p - 1) + a + 1)
                copy(yd[:, a, :], bank(V_BANK), s_yd)

            def attention_input(p):
                act.wait_ge(s_xTp, p + 1)
                if p >= 1:
                    act.wait_ge(s_qkv, 2 * p)
                    act.wait_ge(s_xTlo, p)
                copy(xT_hi[:], x_bank(), s_xThi)

            def keys(p):
                act.wait_ge(s_kTp, p + 1)
                if p == 0:
                    act.wait_ge(s_init, 2)
                else:
                    act.wait_ge(s_score, 8 * p)
                kT = bank(V_BANK).rearrange("p (a r t) -> p a r t", a=2, r=2)
                kp = kpad.rearrange("p a (r o) t -> p a r o t", o=2)
                copy(kp[0:64, :, :, 0, :], kT[0:64], s_kT)
                copy(kp[64:128, :, :, 1, :], kT[64:128], s_kT)

            def squares_and_values(p):
                act.wait_ge(s_qkv, 2 * (p + 1))
                if p >= 1:
                    act.wait_ge(s_nred, p)
                nc.scalar.activation(sq[:], qk_ps, ACT.Square).then_inc(s_sq, 1)
                if p >= 2:
                    act.wait_ge(s_pv, 2 * (p - 1))
                if p == 0:
                    act.wait_ge(s_init, 2)
                copy(vz_v[:, p % 2, :, :, 0:HD], v_ps, s_v)

            def roots(p):
                act.wait_ge(s_norm, NORM_STEPS * p + 1)
                nc.scalar.activation(lnss[:], ss[:], ACT.Ln).then_inc(s_root, 1)
                act.wait_ge(s_root, 2 * p + 1)
                nc.scalar.activation(nrm[:], lnss[:], ACT.Exp, scale=0.5).then_inc(s_root, 1)

            def expert_input(p, n):
                act.wait_ge(s_x2Tp, p + 1)
                if p >= 1:
                    act.wait_ge(s_gate, p)
                copy(x2T[:], x_bank(n), s_x2T)

            def projection_input(p):
                act.wait_ge(s_yTp, p + 1)
                if p >= 1:
                    act.wait_ge(s_proj, 2 * p)
                    act.wait_ge(s_yTlo, p)
                copy(yT_hi[:], x_bank(), s_yThi)

            def high_queries(p):
                act.wait_ge(s_stage, STAGE_STEPS * p + 2)
                if p >= 2:
                    act.wait_ge(s_qTp, 4 * (p - 1))
                copy(q_stage(p % 2)[0], bc(q_n, 2, 2), s_qhi)

            attention_input(0)
            squares_and_values(0)
            attention_input(1)
            roots(0)
            high_queries(0)
            for i in range(PAIRS):
                q_copies(i, 0)
                keys(i)
                if live(i + 1) and i >= 1:
                    attention_input(i + 1)
                probabilities(i, 0, range(0, 2))
                if live(i + 1):
                    squares_and_values(i + 1)
                probabilities(i, 0, range(2, KVH))
                if live(i - 2):
                    expert_input(i - 2, X_BANK)
                if live(i + 1):
                    roots(i + 1)
                q_copies(i, 1)
                outputs(i, 0)
                probabilities(i, 1, range(0, 2))
                if live(i + 1):
                    high_queries(i + 1)
                probabilities(i, 1, range(2, KVH))
                if i == 0:
                    act.wait_ge(s_filled, 4)
                    act.dma_start(x_rows[EXPERTS * CAP:, :].rearrange("(n p) c -> p n c", p=P),
                                  bc(pad_rows[:], SPARE, 1)).then_inc(s_pads, 16)
                parts, c = (w1_f, w2_f)[i // PIECES], i % PIECES
                act.wait_ge((s_w1raw, s_w2raw)[i // PIECES], 16 * KC)
                copy(parts[0][:, c * PIECE:(c + 1) * PIECE], raw_f[:, c * PIECE:(c + 1) * PIECE], s_split_hi)
                outputs(i, 1)
                if live(i - 1):
                    projection_input(i - 1)
            projection_input(PAIRS - 1)
            expert_input(PAIRS - 2, S_BANK)
            expert_input(PAIRS - 1, S_BANK + 1)
            write_padding(act, 4, EXPERTS)

            def slot_copy(dst, n, done):
                copy(dst, ps[:, n, 0:D].rearrange("p (k t) -> p k t", k=KC), done)

            def rows_high(s, b, reused=True):
                act.wait_ge(s_sxp, s + 1)
                if reused:
                    act.wait_ge(s_up, s - 1)
                    act.wait_ge(s_sxlo, s - 1)
                slot_copy(xT_hi[:, :, b, :], b, s_sxhi)

            def hidden_high(s, b, reused=True):
                act.wait_ge(s_hTp, s + 1)
                if reused:
                    act.wait_ge(s_down, s - 1)
                    act.wait_ge(s_hTlo, s - 1)
                nc.scalar.activation(yT_hi[:, :, b, :], ps[:, 4 + b, 0:D].rearrange("p (k t) -> p k t", k=KC),
                                     ACT.Relu).then_inc(s_hThi, 1)

            for s in range(2):
                rows_high(s, s, reused=False)
            for s in range(2):
                rows_high(s + 2, s)
                hidden_high(s, s, reused=False)
            whole = SLOTS - 2 - SLOTS % 2
            with act.Fori(2, whole, 2) as s:
                for b in range(2):
                    rows_high(s + b + 2, b)
                    hidden_high(s + b, b)
            for s in range(whole, SLOTS):
                if s + 2 < SLOTS:
                    rows_high(s + 2, s % 2)
                hidden_high(s, s % 2)

            for t in range(0, SEQS, 2):
                act.wait_ge(s_mix, 2 * (t + 2))
                act.dma_start(out.rearrange("t p d -> p t d")[:, t:t + 2], h[:, t:t + 2, :]).then_inc(s_out, 16)
            act.wait_ge(s_out, 16 * PAIRS)

        @block.vector
        def _(dve):
            V = nc.vector

            def lo_part(dst, n, hi, done):
                V.tensor_tensor(dst, ps[:, n, :].rearrange("p (k a t) -> p k a t", k=KC, a=2), hi.bitcast(F32),
                                ALU.subtract).then_inc(done, 1)

            dve.wait_ge(s_wraw, 32)
            for n, (hi, lo, a, b) in enumerate(((wq_hi, wq_lo, 0, KC * QKV), (wp_hi, wp_lo, KC * QKV, KC * (QKV + D)))):
                V.tensor_copy(hi.rearrange("p k n -> p (k n)"), raw_f[:, a:b]).then_inc(s_hi, 1)
                dve.wait_ge(s_hi, 2 * n + 1)
                V.tensor_tensor(lo.rearrange("p k n -> p (k n)"), raw_f[:, a:b],
                                hi.rearrange("p k n -> p (k n)").bitcast(F32), ALU.subtract).then_inc(s_hi, 1)
            V.memset(seen[:], 0.0).then_inc(s_seen0, 1)
            for b in range(2):
                V.memset(q_stage(b)[2].bitcast(F32), 0.0).then_inc(s_blank, 1)

            def low_weights(parts, c, high):
                a, b = c * PIECE, (c + 1) * PIECE
                dve.wait_ge(s_split_hi, high)
                V.tensor_tensor(parts[1][:, a:b], raw_f[:, a:b], parts[0][:, a:b].bitcast(F32), ALU.subtract).then_inc(s_split, 2)

            def statistics(src, bn_, mv_, var_, eps, steps, base):
                for a in range(2):
                    V.bn_stats(bn_[:, a, :], src(a)).then_inc(steps, 1)
                for a in range(2):
                    dve.wait_ge(steps, base + 1 + a)
                    V.bn_aggr(mv_[:, a, :], bn_[:, a, :]).then_inc(steps, 1)
                dve.wait_ge(steps, base + 4)
                V.tensor_scalar(var_[:], mv_[:, :, 1], eps, None, ALU.add).then_inc(steps, 1)

            def embedding_norms(p, step):
                base = LN_STEPS * p
                pair = h[:, 2 * p:2 * p + 2, :]
                if step == 0:
                    for a in range(2):
                        dve.wait_ge(s_emb[2 * p + a], 16)
                    statistics(lambda a: pair[:, a, :], bn, mv, var_e, TOK_EPS, s_ln, base)
                if step == 1:
                    if p == 0:
                        dve.wait_ge(s_const, 16 * 6)
                    for a in range(2):
                        V.scalar_tensor_tensor(pair[:, a, :], pair[:, a, :], mv[:, a, 0:1], gam[:], ALU.subtract,
                                               ALU.mult).then_inc(s_ln, 1)
                if step in (2, 3):
                    a = step - 2
                    dve.wait_ge(s_rstd, 2 * p + 1)
                    dve.wait_ge(s_ln, base + 6 + a)
                    V.scalar_tensor_tensor(pair[:, a, :], pair[:, a, :], rstd[:, a:a + 1], bet[:], ALU.mult,
                                           ALU.add).then_inc(s_ln, 1)
                if step in (4, 5):
                    a = step - 4
                    dve.wait_ge(s_ln, base + 8 + a)
                    V.bn_stats(bn[:, a, :], pair[:, a, :]).then_inc(s_ln, 1)
                if step == 6:
                    for a in range(2):
                        dve.wait_ge(s_ln, base + 10 + a)
                        V.bn_aggr(mv[:, a, :], bn[:, a, :]).then_inc(s_ln, 1)
                    dve.wait_ge(s_ln, base + 13)
                    V.tensor_scalar(var_e[:], mv[:, :, 1], LN_EPS, None, ALU.add).then_inc(s_ln, 1)
                if step == 7:
                    dve.wait_ge(s_rstd, 2 * p + 2)
                    if p >= 2:
                        dve.wait_ge(s_xTp, p - 1)
                    for a in range(2):
                        V.tensor_scalar(xn[:, p % 2, a, :], pair[:, a, :], mv[:, a, 0:1], rstd[:, a:a + 1],
                                        ALU.subtract, ALU.mult).then_inc(s_xn, 1)

            cos = bc(bc(cf[:, C_COS:C_COS + HD], HEADS + KVH, 1), 2, 1)
            sin_a = bc(bc(cf[:, C_SIN:C_SIN + HD // 2], HEADS + KVH, 1), 2, 1)
            sin_b = bc(bc(cf[:, C_SIN + HD // 2:C_SIN + HD], HEADS + KVH, 1), 2, 1)
            heads = lambda ap: ap.rearrange("p a (s d) -> p a s d", d=HD)

            def guard(p):
                dve.wait_ge(s_nred, p + 1)
                V.tensor_scalar(ss[:], ss[:], 1e-18, None, ALU.max).then_inc(s_norm, 1)

            def rotate(p):
                dve.wait_ge(s_v, p + 1)
                if p >= 1:
                    dve.wait_ge(s_qlo, p)
                V.tensor_tensor(heads(qcos[:]), heads(qk_ps), cos, ALU.mult).then_inc(s_rope, 1)
                guard(p)
                V.tensor_tensor(heads(qsin[:])[:, :, :, 0:8], heads(qk_ps)[:, :, :, 8:16], sin_a, ALU.mult).then_inc(s_rope, 1)
                V.tensor_tensor(heads(qsin[:])[:, :, :, 8:16], heads(qk_ps)[:, :, :, 0:8], sin_b, ALU.mult).then_inc(s_rope, 1)
            def squared_norms(p):
                dve.wait_ge(s_sq, p + 1)
                V.tensor_reduce(ss[:], sq.rearrange("p a (s d) -> p (a s) d", d=HD), AX_X, ALU.add).then_inc(s_nred, 1)

            def heron(p, step):
                dve.wait_ge(s_norm, NORM_STEPS * p + 1 + step)
                if step == 0:
                    dve.wait_ge(s_root, 2 * p + 2)
                    ins = V.reciprocal(inv[:], nrm[:])
                if step == 1:
                    ins = V.tensor_tensor(inv[:], inv[:], ss[:], ALU.mult)
                if step == 2:
                    ins = V.tensor_tensor(inv[:], inv[:], nrm[:], ALU.add)
                if step == 3:
                    ins = V.tensor_scalar(inv[:], inv[:], 0.5, NORM_EPS, ALU.mult, ALU.add)
                if step == 4:
                    ins = V.reciprocal(rn[:], inv[:])
                ins.then_inc(s_norm, 1)

            def stage(p):
                dve.wait_ge(s_norm, NORM_STEPS * (p + 1))
                dve.wait_ge(s_add, p + 1)
                rn_v = bc(rn.rearrange("p (a s) -> p a s", a=2), HD, 3)
                V.tensor_tensor(k_n.rearrange("p (a s) d -> p a s d", a=2), heads(qcos[:])[:, :, HEADS:], rn_v[:, :, HEADS:],
                                ALU.mult).then_inc(s_stage, 1)
                V.tensor_tensor(q_n.rearrange("p (a s) d -> p a s d", a=2), heads(qcos[:])[:, :, 0:HEADS], rn_v[:, :, 0:HEADS],
                                ALU.mult).then_inc(s_stage, 1)
                base = STAGE_STEPS * p
                b = p % 2
                if p >= 2:
                    dve.wait_ge(s_kTp, p - 1)
                k = bc(k_n, 2, 2)
                kv = kst[:, b].rearrange("p a g (l c d) -> p (a g) l c d", l=2, c=2)
                dve.wait_ge(s_stage, base + 1)
                V.tensor_copy(kv[:, :, 0], k).then_inc(s_stage, 1)
                dve.wait_ge(s_stage, base + 3)
                V.tensor_tensor(kv[:, :, 1], k, kv[:, :, 0].bitcast(F32), ALU.subtract).then_inc(s_stage, 1)

            def normalise_outputs(p):
                dve.wait_ge(s_ydT, 2 * (p + 1))
                V.reciprocal(rden.rearrange("p (a s) -> p a s", a=2), y_ps[:, :, :, HD]).then_inc(s_y, 1)
                dve.wait_ge(s_y, 2 * p + 1)
                if p >= 1:
                    dve.wait_ge(s_yTp, p)
                V.tensor_tensor(heads(y[:]), y_ps[:, :, :, 0:HD], bc(rden.rearrange("p (a s) -> p a s", a=2), HD, 3),
                                ALU.mult).then_inc(s_y, 1)

            def residual(p):
                dve.wait_ge(s_proj, 2 * (p + 1))
                x = h[:, 2 * p:2 * p + 2, :]
                V.tensor_tensor(x, x, ps[:, QKV_BANK, :].rearrange("p (a d) -> p a d", a=2), ALU.add).then_inc(s_res, 1)

            def residual_statistics(p):
                dve.wait_ge(s_res, p + 1)
                statistics(lambda a: h[:, 2 * p + a, :], bn3, mv3, var3, LN_EPS, s_ln3, 5 * p)

            def expert_input(p):
                dve.wait_ge(s_rstd3, p + 1)
                if p >= RBUF:
                    dve.wait_ge(s_scat[p % RBUF], 16 * 2 * TOPK * (p // RBUF))
                for a in range(2):
                    V.tensor_scalar(rows[:, 2 * (p % RBUF) + a, 0:D], h[:, 2 * p + a, :], mv3[:, a, 0:1], rstd3[:, a:a + 1],
                                    ALU.subtract, ALU.mult).then_inc(s_x2, 1)

            def route(p, n):
                base, r = ROUTE_STEPS * p, 2 * (p % RBUF)
                dve.wait_ge(s_gate, p + 1)
                V.tensor_tensor(sco[:], ps[:, n, 0:2 * EXPERTS].rearrange("p (a e) -> p a e", a=2),
                                bc(bg[:], 2, 1), ALU.add).then_inc(s_route, 1)
                dve.wait_ge(s_route, base + 1)
                for a in range(2):
                    V.max(top[:, 2 * p + a, :], sco[:, a, :]).then_inc(s_route, 1)
                for a in range(2):
                    dve.wait_ge(s_route, base + 2 + a)
                    V.max_index(topi[:, a, :], top[:, 2 * p + a, :], sco[:, a, :]).then_inc(s_route, 1)
                dve.wait_ge(s_route, base + 5)
                V.tensor_copy(topf[:], topi[:, :, 0:TOPK]).then_inc(s_route, 1)
                V.tensor_copy(rows[:, r:r + 2, D], cf[:, C_TOK + 2 * p:C_TOK + 2 * p + 2]).then_inc(s_route, 1)
                V.tensor_copy(rows[:, r:r + 2, D + 1], topi[:, :, 0]).then_inc(s_route, 1)
                dve.wait_ge(s_route, base + 6)
                ids = bc(bc(cf[:, C_EID:C_EID + EXPERTS], TOPK, 1), 2, 1)
                V.tensor_tensor(pick[:], ids, bc(topf[:], EXPERTS, 3), ALU.is_equal).then_inc(s_route, 1)
                cbase = CHOSEN_STEPS * p
                if p == 0:
                    dve.wait_ge(s_seen0, 1)
                else:
                    dve.wait_ge(s_before, p)
                    V.tensor_tensor(seen[:, 0, :], seen[:, 1, :], chosen[:, 1, :], ALU.add).then_inc(s_seen0, 1)
                    dve.wait_ge(s_seen0, p + 1)
                dve.wait_ge(s_route, base + 9)
                V.tensor_tensor(chosen[:], pick[:, :, 0, :], pick[:, :, 1, :], ALU.add).then_inc(s_chosen, 1)
                dve.wait_ge(s_chosen, cbase + 1)
                V.tensor_tensor(seen[:, 1, :], seen[:, 0, :], chosen[:, 0, :], ALU.add).then_inc(s_chosen, 1)

            def places(p, n):
                dve.wait_ge(s_before, p + 1)
                V.tensor_tensor(place[:], ps[:, n, 0:2 * EXPERTS].rearrange("p (a e) -> p a e", a=2),
                                bc(cf[:, C_ECAP:C_ECAP + EXPERTS], 2, 1), ALU.add).then_inc(s_place, 1)
                dve.wait_ge(s_place, p + 1)
                V.tensor_tensor(picked[:], pick[:], bc(place[:], TOPK, 2), ALU.mult).then_inc(s_picked, 1)
                dve.wait_ge(s_picked, 2 * p + 1)
                V.tensor_reduce(destf[:], picked[:], AX_X, ALU.add).then_inc(s_picked, 1)
                dve.wait_ge(s_picked, 2 * p + 2)
                V.tensor_copy(dest[:, 2 * p:2 * p + 2, :], destf[:]).then_inc(s_dest, 1)

            def projection_input(p):
                dve.wait_ge(s_yThi, p + 1)
                if p >= 1:
                    dve.wait_ge(s_proj, 2 * p)
                lo_part(yT_lo[:], X_BANK, yT_hi[:], s_yTlo)

            def attention_input(p):
                dve.wait_ge(s_xThi, p + 1)
                if p >= 1:
                    dve.wait_ge(s_qkv, 2 * p)
                lo_part(xT_lo[:], X_BANK, xT_hi[:], s_xTlo)

            for step in range(8):
                embedding_norms(0, step)
            for step in range(2):
                embedding_norms(1, step)
            attention_input(0)
            for step in range(2, 8):
                embedding_norms(1, step)
            squared_norms(0)
            rotate(0)
            attention_input(1)
            for step in range(5):
                heron(0, step)
            stage(0)
            for i in range(PAIRS):
                p = i + 1
                if live(i - 2):
                    residual(i - 2)
                if live(p) and p >= 2:
                    attention_input(p)
                if live(i - 2):
                    residual_statistics(i - 2)
                if live(i + 2):
                    embedding_norms(i + 2, 0)
                if live(i - 2):
                    expert_input(i - 2)
                if live(i - 1):
                    normalise_outputs(i - 1)
                if live(i + 2):
                    embedding_norms(i + 2, 1)
                if live(p):
                    squared_norms(p)
                    rotate(p)
                for step in range(5):
                    if live(p):
                        heron(p, step)
                    if live(i + 2):
                        embedding_norms(i + 2, step + 2)
                if live(p):
                    stage(p)
                if live(i - 2):
                    route(i - 2, X_BANK)
                if live(i + 2):
                    embedding_norms(i + 2, 7)
                if live(i - 2):
                    places(i - 2, X_BANK)
                if live(i - 1):
                    projection_input(i - 1)
                if i < PIECES:
                    low_weights(w1_f, i, i + 1)
            normalise_outputs(PAIRS - 1)
            residual(PAIRS - 2)
            residual_statistics(PAIRS - 2)
            projection_input(PAIRS - 1)
            expert_input(PAIRS - 2)
            residual(PAIRS - 1)
            residual_statistics(PAIRS - 1)
            expert_input(PAIRS - 1)
            route(PAIRS - 2, S_BANK)
            places(PAIRS - 2, S_BANK)
            route(PAIRS - 1, S_BANK + 1)
            places(PAIRS - 1, S_BANK + 1)

            steps = [0]

            def table(ins):
                ins.then_inc(s_table, 1)
                steps[0] += 1
                dve.wait_ge(s_table, steps[0])

            slots = cf[:, C_SLOT:C_SLOT + SLOTS]
            dve.wait_ge(s_before_all, 1)
            V.tensor_copy(cnt[:], ps[:, X_BANK, 0:EXPERTS]).then_inc(s_cnt, 1)
            dve.wait_ge(s_cnt, 1)
            V.tensor_tensor(pad_row[:], cnt[:], cf[:, C_ECAP:C_ECAP + EXPERTS], ALU.add).then_inc(s_padrow, 1)
            table(V.tensor_tensor(over[:], bc(cnt[:], SEQS, 2), bc(cf[:, C_THR:C_THR + SEQS], EXPERTS, 1), ALU.is_gt))
            table(V.tensor_reduce(tiles[:], over[:], AX_X, ALU.add))
            tri = cf[:, C_TRI:C_TRI + EXPERTS * EXPERTS].rearrange("p (a b) -> p a b", a=EXPERTS)
            table(V.tensor_tensor(before_e[:], bc(tiles[:], EXPERTS, 1), tri, ALU.mult))
            table(V.tensor_reduce(ends[:], before_e[:], AX_X, ALU.add))
            table(V.tensor_tensor(past[:], bc(slots, EXPERTS, 2), bc(ends[:], SLOTS, 1), ALU.is_ge))
            table(V.tensor_reduce(slot_e[:], past[:], AX_X, ALU.add))
            table(V.tensor_tensor(past_n[:], past[:], bc(tiles[:], SLOTS, 1), ALU.mult))
            table(V.tensor_reduce(slot_0[:], past_n[:], AX_X, ALU.add))
            table(V.tensor_tensor(slot_0[:], slots, slot_0[:], ALU.subtract))
            table(V.tensor_scalar(slot_r[:], slot_e[:], float(CAP), None, ALU.mult))
            table(V.scalar_tensor_tensor(slot_row[:], slot_0[:], float(P), slot_r[:], ALU.mult, ALU.add))
            table(V.tensor_scalar(slot_col[:], slot_e[:], float(EXPERTS - 1), float(D), ALU.min, ALU.mult))
            assert steps[0] == TABLE_STEPS

            for c in range(PIECES):
                low_weights(w2_f, c, PIECES + c + 1)

            def slot_lo(dst, n, hi, done):
                V.tensor_tensor(dst, ps[:, n, 0:D].rearrange("p (k t) -> p k t", k=KC), hi.bitcast(F32),
                                ALU.subtract).then_inc(done, 1)

            dve.wait_ge(s_bias, 32)
            column = SlotValues(nc, slot_col, mybir.EngineType.DVE, (EXPERTS - 1) * D)
            for s in range(-2, SLOTS + 1):
                if s + 2 < SLOTS:
                    m = s + 2
                    dve.wait_ge(s_sxhi, m + 1)
                    if m >= 2:
                        dve.wait_ge(s_up, m - 1)
                    slot_lo(xT_lo[:, :, m % 2, :], m % 2, xT_hi[:, :, m % 2, :], s_sxlo)
                if 0 <= s + 1 < SLOTS:
                    m = s + 1
                    n = m % TBUF
                    V.tensor_tensor(second[:, n:n + 1], slot_x[:, m % XBUF, D + 1:D + 2], slot_e[:, bass.ds(m, 1)],
                                    ALU.not_equal).then_inc(s_isk, 1)
                    dve.wait_ge(s_up, m + 1)
                    if m >= 2:
                        dve.wait_ge(s_hTp, m - 1)
                    V.tensor_tensor(hid[:, m % 2, :], ps[:, 2 + m % 2, 0:D], b1_f[:, bass.ds(column(m), D)],
                                    ALU.add).then_inc(s_hid, 1)
                    dve.wait_ge(s_isk, m + 1)
                    V.scalar_tensor_tensor(to_row[:, n:n + 1], second[:, n:n + 1], float(TOKENS),
                                           slot_x[:, m % XBUF, D:D + 1], ALU.mult, ALU.add).then_inc(s_to, 1)
                if 0 <= s < SLOTS:
                    b = s % 2
                    dve.wait_ge(s_hThi, s + 1)
                    if s >= 2:
                        dve.wait_ge(s_down, s - 1)
                    V.scalar_tensor_tensor(yT_lo[:, :, b, :], ps[:, 4 + b, 0:D].rearrange("p (k t) -> p k t", k=KC), 0.0,
                                           yT_hi[:, :, b, :].bitcast(F32), ALU.max, ALU.subtract).then_inc(s_hTlo, 1)
                if s >= 1:
                    m = s - 1
                    dve.wait_ge(s_down, m + 1)
                    if m >= YBUF:
                        dve.wait_ge(s_sent[m % YBUF], 16 * (m // YBUF))
                    V.tensor_tensor(slot_y[:, m % YBUF, :], ps[:, 6 + m % 2, 0:D], b2_f[:, bass.ds(column(m), D)],
                                    ALU.add).then_inc(s_ys, 1)

            for t in range(0, SEQS, 2):
                for k in range(TOPK):
                    for u in (t, t + 1):
                        if k == 0:
                            dve.wait_ge(s_back[u % CBUF], 16 * (u // CBUF + 1))
                        else:
                            dve.wait_ge(s_mix, 2 * t + 1 + u - t)
                        V.scalar_tensor_tensor(h[:, u, :], coming[:, u % CBUF, k, :], top[:, u, k:k + 1], h[:, u, :],
                                               ALU.mult, ALU.add).then_inc(s_mix, 1)


def constants():
    cf = np.zeros((P, C_WIDTH), np.float32)
    cf[:, C_ID:C_ID + P] = np.eye(P)
    theta = (1.0 / np.float32(10000.0) ** (np.arange(0, HD, 2, dtype=np.float32) / np.float32(HD))).astype(np.float32)
    angle = np.arange(P, dtype=np.float32)[:, None] * theta
    cf[:, C_COS:C_COS + HD] = np.tile(np.cos(angle), 2)
    cf[:, C_SIN:C_SIN + HD] = np.concatenate([-np.sin(angle), np.sin(angle)], 1)
    cf[:, C_ECAP:C_ECAP + EXPERTS] = np.arange(EXPERTS) * CAP
    cf[:, C_EID:C_EID + EXPERTS] = np.arange(EXPERTS)
    cf[:, C_SLOT:C_SLOT + SLOTS] = np.arange(SLOTS)
    cf[:, C_THR:C_THR + SEQS] = np.arange(SEQS) * P
    cf[:, C_TRI:C_TRI + EXPERTS * EXPERTS] = np.tril(np.ones((EXPERTS, EXPERTS))).ravel()
    cf[:, C_TOK:C_TOK + SEQS] = np.arange(SEQS) * P + np.arange(P)[:, None]
    cb = np.zeros((P, B_WIDTH), np.float32)
    cb[:, B_ID:B_ID + P] = np.eye(P)
    cb[:, B_BEFORE:B_BEFORE + P] = np.triu(np.ones((P, P)), 1)
    cb[:, B_ONES:B_ONES + P] = 1.0
    cb[:, B_MASK:] = np.tile(np.where(np.arange(P)[:, None] > np.arange(P), MASKED, 0.0), REP)
    return cf, cb.astype(mybir.dt.np(BF16))


def kernel(**inputs):
    import concourse.bacc as bacc
    from concourse.bass_utils import run_bass_kernel_spmd as run

    a = {k: np.asarray(v) for k, v in inputs.items()}
    wq = a["L0_attn_Wq"].reshape(KVH, REP, HD, D).transpose(1, 0, 2, 3).reshape(D, D)
    w_qkv = np.concatenate([wq, a["L0_attn_Wkv"]], 0).T
    w_proj = a["L0_attn_Wproj"].T.reshape(KVH, REP, HD, D).transpose(1, 0, 2, 3).reshape(D, D)
    cf, cb = constants()
    arrays = {
        "x_idx": a["x"].T, "seg_idx": a["mask_BS_i2_0"].T, "w_word": a["L0_tok_W_word"], "w_pos": a["L0_tok_W_pos"],
        "w_seg": a["L0_tok_W_seg"], "gamma": a["L0_tok_gamma"], "beta": a["L0_tok_beta"], "w_qkv": w_qkv,
        "w_proj": w_proj, "w_gate": a["L0_ffn_W_gate"], "b_gate": a["L0_ffn_b_gate"], "w1": a["L0_ffn_W1"],
        "b1": a["L0_ffn_b1"], "w2": a["L0_ffn_W2"], "b2": a["L0_ffn_b2"], "consts": cf, "consts_bf": cb,
    }
    arrays = {k: np.ascontiguousarray(v) for k, v in arrays.items()}
    nc = bacc.Bacc("TRN2", target_bir_lowering=False, num_devices=1)
    args = [nc.dram_tensor(k, v.shape, mybir.dt.from_np(v.dtype), kind="ExternalInput").ap() for k, v in arrays.items()]
    out = nc.dram_tensor("out", (SEQS, P, D), F32, kind="ExternalOutput").ap()
    attention_moe_program(nc, *args, out)
    result = run(nc, [arrays], core_ids=[0])
    return result.results[0]["out"]
```
